# Optimizing a Trainium2 kernel written in Bass

```python
import numpy as np
import jax
import jax.numpy as jnp

def _softmax(x, axis=-1):
    return jax.nn.softmax(x, axis=axis)

def _gelu(x):
    return jax.nn.gelu(x, approximate=True)

def _silu(x):
    return jax.nn.silu(x)

def _sigmoid(x):
    return jax.nn.sigmoid(x)

def _layernorm(x, axis=-1, eps=1e-05):
    m = jnp.mean(x, axis=axis, keepdims=True)
    v = jnp.var(x, axis=axis, keepdims=True)
    return (x - m) / jnp.sqrt(v + eps)

def _scatter_add(tgt, idx, src, axis=0):
    return tgt.at[idx].add(src)

def _segment_sum(src, seg, n):
    return jax.ops.segment_sum(src, seg, n)
kernel_name = 'mk_flamingo_gated_d1_seqx_r8_1ac321'

def setup_inputs(seed: int=0):
    np.random.seed(seed)
    _w = jnp.asarray

    def _rec_inputs():
        import jax
        import jax.numpy as jnp
        _rk = jax.random.key(seed)
        x = -0.0002928 + 1 * jax.random.normal(jax.random.fold_in(_rk, 1), (8, 128, 256), jnp.float32)
        _lenS = 128 - jax.random.randint(jax.random.fold_in(_rk, 7), (8,), 0, max(1, 128 // 4) + 1, jnp.int32)
        _lenS2 = 128 - jax.random.randint(jax.random.fold_in(_rk, 8), (8,), 0, max(1, 128 // 4) + 1, jnp.int32)
        _ctx_2048P = jax.random.normal(jax.random.fold_in(_rk, 11), (8, 16, 256), jnp.float32)
        _ctx_2048c = jax.random.dirichlet(jax.random.fold_in(_rk, 511), 0.3 * jnp.ones((16,), jnp.float32), (8, 128))
        _ctx_2048t = jnp.einsum('bsk,bkd->bsd', _ctx_2048c, _ctx_2048P)
        _ctx_2048t = _ctx_2048t * jax.lax.rsqrt(jnp.mean(jnp.square(_ctx_2048t)) + 1e-12) * 0.953939
        ctx_2048 = -1.39393e-06 + 0.999914 * (_ctx_2048t + 0.3 * jax.random.normal(jax.random.fold_in(_rk, 611), (8, 128, 256), jnp.float32))
        _g = jax.random.normal(jax.random.fold_in(_rk, 9001), (2, 1), jnp.float32)
        _g = jnp.sign(_g) * jnp.maximum(jnp.abs(_g), 1.0) + (_g == 0) * 1.0
        g_xattn = _g[0]
        g_ffn = _g[1]
        return (x, ctx_2048, g_xattn, g_ffn)
    x, ctx_2048, g_xattn, g_ffn = _rec_inputs()

    def _L0_xattn_setup():
        import math
        import jax, jax.numpy as jnp
        import numpy as np
        N_HEADS = 16
        key = jax.random.key(seed)
        k1, k2 = jax.random.split(key)
        qkv = jax.random.normal(k1, (2, 128, 256), dtype=jnp.float32)
        y = jax.random.normal(k2, (2, 128, 256), dtype=jnp.float32)
        return {'qkv': qkv, 'y': y}
    _L0_xattn_all = _L0_xattn_setup()
    _L0_xattn_in = {k: v for k, v in _L0_xattn_all.items() if k in ()}
    del _L0_xattn_all

    def _L0_ffn_setup():
        import jax, jax.numpy as jnp
        import numpy as np
        N_EXPERTS = 8
        TOP_K = 2
        N_GROUP = 4
        TOPK_GROUP = 2
        ROUTED_SCALE = 1.0

        def _group_limited_topk(scores):
            T, N = scores.shape
            E = N // N_GROUP
            group_scores = scores.reshape(T, N_GROUP, E).max(axis=-1)
            _, gidx = jax.lax.top_k(group_scores, TOPK_GROUP)
            gmask = jax.nn.one_hot(gidx, N_GROUP, dtype=scores.dtype).sum(1)
            smask = jnp.repeat(gmask, E, axis=1)
            masked = jnp.where(smask > 0, scores, jnp.zeros((), scores.dtype))
            topk_w, topk_i = jax.lax.top_k(masked, TOP_K)
            return (topk_w, topk_i)
        key = jax.random.key(seed)
        ks = jax.random.split(key, 8)
        B, S, H, F, FS, N = (2, 128, 256, 176, 352, N_EXPERTS)
        std = jnp.float32(0.02)
        return {'hidden_states': jax.random.normal(ks[0], (B, S, H), jnp.float32), 'gate_weight': jax.random.normal(ks[1], (N, H), jnp.float32) * std, 'gate_w': jax.random.normal(ks[2], (N, F, H), jnp.float32) * std, 'up_w': jax.random.normal(ks[3], (N, F, H), jnp.float32) * std, 'down_w': jax.random.normal(ks[4], (N, H, F), jnp.float32) * std, 'sh_gate_w': jax.random.normal(ks[5], (FS, H), jnp.float32) * std, 'sh_up_w': jax.random.normal(ks[6], (FS, H), jnp.float32) * std, 'sh_down_w': jax.random.normal(ks[7], (H, FS), jnp.float32) * std}
    _L0_ffn_all = _L0_ffn_setup()
    _L0_ffn_in = {k: v for k, v in _L0_ffn_all.items() if k in ('gate_weight', 'gate_w', 'up_w', 'down_w', 'sh_gate_w', 'sh_up_w', 'sh_down_w')}
    del _L0_ffn_all
    return {'x': x, 'ctx_2048': ctx_2048, 'g_xattn': g_xattn, 'g_ffn': g_ffn, 'L0_ffn_gate_weight': _L0_ffn_in['gate_weight'], 'L0_ffn_gate_w': _L0_ffn_in['gate_w'], 'L0_ffn_up_w': _L0_ffn_in['up_w'], 'L0_ffn_down_w': _L0_ffn_in['down_w'], 'L0_ffn_sh_gate_w': _L0_ffn_in['sh_gate_w'], 'L0_ffn_sh_up_w': _L0_ffn_in['sh_up_w'], 'L0_ffn_sh_down_w': _L0_ffn_in['sh_down_w']}

def reference(x, ctx_2048, g_xattn, g_ffn, L0_ffn_gate_weight, L0_ffn_gate_w, L0_ffn_up_w, L0_ffn_down_w, L0_ffn_sh_gate_w, L0_ffn_sh_up_w, L0_ffn_sh_down_w):
    import jax
    import jax.numpy as jnp

    def _L0_xattn_ref(qkv, y):
        import math
        import jax, jax.numpy as jnp
        import numpy as np
        N_HEADS = 16
        bs, width, length = qkv.shape
        ch = width // N_HEADS
        q = qkv.reshape(bs * N_HEADS, ch, length)
        k = v = y.reshape(bs * N_HEADS, ch, -1)
        scale = 1.0 / math.sqrt(math.sqrt(ch))
        weight = jnp.einsum('bct,bcs->bts', q * scale, k * scale)
        weight = jax.nn.softmax(weight.astype(jnp.float32), axis=-1).astype(weight.dtype)
        a = jnp.einsum('bts,bcs->bct', weight, v)
        return a.reshape(bs, -1, length)

    def _L0_ffn_ref(hidden_states, gate_weight, gate_w, up_w, down_w, sh_gate_w, sh_up_w, sh_down_w):
        import jax, jax.numpy as jnp
        import numpy as np
        N_EXPERTS = 8
        TOP_K = 2
        N_GROUP = 4
        TOPK_GROUP = 2
        ROUTED_SCALE = 1.0

        def _group_limited_topk(scores):
            T, N = scores.shape
            E = N // N_GROUP
            group_scores = scores.reshape(T, N_GROUP, E).max(axis=-1)
            _, gidx = jax.lax.top_k(group_scores, TOPK_GROUP)
            gmask = jax.nn.one_hot(gidx, N_GROUP, dtype=scores.dtype).sum(1)
            smask = jnp.repeat(gmask, E, axis=1)
            masked = jnp.where(smask > 0, scores, jnp.zeros((), scores.dtype))
            topk_w, topk_i = jax.lax.top_k(masked, TOP_K)
            return (topk_w, topk_i)
        B, S, H = hidden_states.shape
        h = hidden_states.reshape(-1, H)
        logits = h.astype(jnp.float32) @ gate_weight.astype(jnp.float32).T
        scores = jax.nn.softmax(logits, axis=-1)
        topk_w, topk_i = _group_limited_topk(scores)
        topk_w = (topk_w * ROUTED_SCALE).astype(h.dtype)
        wmat = (jax.nn.one_hot(topk_i, N_EXPERTS, dtype=topk_w.dtype) * topk_w[..., None]).sum(axis=1)
        g = jnp.einsum('th,nfh->ntf', h, gate_w)
        u = jnp.einsum('th,nfh->ntf', h, up_w)
        e = jnp.einsum('ntf,nhf->nth', jax.nn.silu(g) * u, down_w)
        routed = jnp.einsum('nth,tn->th', e, wmat)
        sg = h @ sh_gate_w.T
        su = h @ sh_up_w.T
        shared = jax.nn.silu(sg) * su @ sh_down_w.T
        return (routed + shared).reshape(B, S, H)
    x = x + jnp.tanh(g_xattn[0]) * _L0_xattn_ref(_layernorm(x, axis=-1), ctx_2048)
    x = x + jnp.tanh(g_ffn[0]) * _L0_ffn_ref(_layernorm(x, axis=-1), L0_ffn_gate_weight, L0_ffn_gate_w, L0_ffn_up_w, L0_ffn_down_w, L0_ffn_sh_gate_w, L0_ffn_sh_up_w, L0_ffn_sh_down_w)
    return x

_drawn_inputs = setup_inputs


def setup_inputs(seed=0):
    import zlib

    import numpy as np

    out = dict(_drawn_inputs(seed))
    spreads = {}
    factors = {'L0_ffn_gate_weight': 8.0,
     'L0_ffn_gate_w': 8.0,
     'L0_ffn_up_w': 8.0,
     'L0_ffn_down_w': 8.0,
     'L0_ffn_sh_gate_w': 3.933,
     'L0_ffn_sh_up_w': 3.893,
     'L0_ffn_sh_down_w': 3.901}
    for name, (base, spread) in spreads.items():
        noise = np.random.default_rng([zlib.crc32(name.encode()), seed]).standard_normal(out[name].shape)
        drawn = base * np.exp(spread * noise) if base else spread * noise
        out[name] = jnp.asarray(drawn.astype(out[name].dtype))
    for name, factor in factors.items():
        out[name] = (out[name] * factor).astype(out[name].dtype)
    return out
```

```python
from contextlib import ExitStack

import concourse.bass as bass
from concourse import mybir

F32 = mybir.dt.float32
F32R = mybir.dt.float32r
ALU = mybir.AluOpType
ACT = mybir.ActivationFunctionType
AX = mybir.AxisListType

B, W, L = 8, 128, 256
HEADS, CH = 16, 8
GROUPS = 4
EXPERTS, FE, FS = 8, 176, 352
F = FS + EXPERTS * FE
NJ = 4
FJ = F // NJ
NC = (F + 127) // 128
FPAD = NC * 128
EPS = 1e-5
PARTS = 3
ROWS = 32 * PARTS
KROWS = ROWS + 2
SLOTS = 16
VCOL = 32
STAGE = (2 * F + EXPERTS) // 3

C_ID, C_MASK, C_L4, C_L8 = 0, 128, 132, 148
C_ALL = 212


def expert_segments(j):
    edges = [0] + [FS + e * FE for e in range(EXPERTS + 1)]
    out = []
    for n in range(EXPERTS + 1):
        a, b = max(edges[n], j * FJ), min(edges[n + 1], (j + 1) * FJ)
        if a < b:
            out.append((a - j * FJ, b - j * FJ, n - 1 if n else None))
    return out


def some(count):
    return not isinstance(count, int) or count > 0


class Step:

    def __init__(self, r, par, new, att, ffn, prep):
        self.r, self.par = r, par
        self.new, self.att, self.ffn, self.prep = new, att, ffn, prep

    def item(self, lag):
        return 2 * self.r + (self.par - lag)

    def buf(self, lag):
        return (self.par - lag) % 2

    def uses(self, lag):
        return self.r + (self.par - lag) // 2


def flamingo_kernel(nc, x, y, yT, gx, gf, wgu, wd, consts, out):
    with ExitStack() as ctx:
        def sb(name, shape, dt=F32):
            return ctx.enter_context(nc.sbuf_tensor(name, shape, dt))

        def ps(name, shape):
            return ctx.enter_context(nc.psum_tensor(name, shape, F32))

        def sem(name):
            return ctx.enter_context(nc.semaphore(name))

        cst = sb("cst", [128, C_ALL])
        ident = cst[:, C_ID:C_ID + 128]
        wguh = sb("wguh", [128, 2, 2 * F + EXPERTS], F32R)
        wgul = sb("wgul", [128, 2, 2 * F + EXPERTS], F32R)
        wdh = sb("wdh", [128, NC, L], F32R)
        wdl = sb("wdl", [128, NC, L], F32R)
        gates = sb("gates", [128, 2])
        tg = sb("tg", [128, 2])
        xs = [sb(f"xs{n}", [ROWS, GROUPS, L]) for n in range(2)]
        kr = [sb(f"kr{n}", [ROWS, GROUPS, L]) for n in range(2)]
        parts = sb("parts", [ROWS, 2, L], F32R)
        qr = parts[64:96, :, :]
        mh, ml = (parts[0:SLOTS, n, :].rearrange("p (c t) -> p c t", t=128) for n in range(2))
        qm = [sb(f"qm{n}", [KROWS, HEADS, L], F32R) for n in range(2)]
        ks = [sb(f"ks{n}", [KROWS, GROUPS, L], F32R) for n in range(2)]
        vraw = sb("vraw", [128, 2, W])
        vt = [sb(f"vt{n}", [128, 2, HEADS, VCOL]) for n in range(2)]
        pst = sb("pst", [ROWS, 2, 2, 6])
        pmv = sb("pmv", [ROWS, 2, 2, 2])
        pve = sb("pve", [ROWS, 2, 2])
        prs = sb("prs", [ROWS, 2, 2])
        mhalf = sb("mhalf", [128, 2])
        zero = sb("zero", [128, 1])
        unused = sb("unused", [1, 1])
        mx = sb("mx", [128, 2, SLOTS])
        probs = sb("probs", [128, 8, 512])
        avsb = sb("avsb", [128, GROUPS, L])
        rec = sb("rec", [128, 2, HEADS])
        aT = sb("aT", [128, 2, HEADS, CH])
        xr = sb("xr", [128, L])
        x1 = sb("x1", [128, L])
        fst = sb("fst", [128, 6])
        fmv = sb("fmv", [128, 2])
        fve = sb("fve", [128, 1])
        frs = sb("frs", [128, 1])
        hTh = sb("hTh", [128, 2, W], F32R)
        hTl = sb("hTl", [128, 2, W], F32R)
        lg = sb("lg", [128, EXPERTS])
        nm = sb("nm", [128, 1])
        e8 = sb("e8", [128, EXPERTS])
        es = sb("es", [128, 1])
        er = sb("er", [128, 1])
        sc = sb("sc", [128, EXPERTS])
        gs = sb("gs", [128, 4])
        cmp4 = sb("cmp4", [128, 3, 4, 4])
        rk4 = sb("rk4", [128, 4])
        m8 = sb("m8", [128, EXPERTS])
        cmp8 = sb("cmp8", [128, 3, 8, 8])
        rk8 = sb("rk8", [128, EXPERTS])
        w8 = sb("w8", [128, EXPERTS])
        thh = sb("thh", [128, STAGE])
        th = thh[:, 0:2 * FJ].rearrange("p (n c) -> p n c", n=2)
        h = thh[:, 2 * FJ:2 * FJ + L]
        tmp = sb("tmp", [128, FJ])
        act_ = sb("act_", [128, FPAD])
        aTh = sb("aTh", [128, NC, W], F32R)
        aTl = sb("aTl", [128, NC, W], F32R)
        yo = sb("yo", [128, L])
        wst = [act_[:, 0:STAGE], thh[:, :]]

        S = [ps(f"S{n}", [128, 2, L]) for n in range(2)]
        ST = [ps(f"ST{n}", [128, 512]) for n in range(2)]
        GU = ps("GU", [128, 2, 512])
        AV = ps("AV", [128, 512])
        M1 = ps("M1", [128, 512])

        const_in = sem("const_in")
        w_in = [sem(f"w_in{n}") for n in range(2)]
        w_hi = sem("w_hi")
        w_lo_dve, w_lo_pool = sem("w_lo_dve"), sem("w_lo_pool")
        x_in = [sem(f"x_in{n}") for n in range(2)]
        y_in = [sem(f"y_in{n}") for n in range(2)]
        mrow_in = [sem(f"mrow_in{n}") for n in range(2)]
        v_in, xr_in, out_done = sem("v_in"), sem("xr_in"), sem("out_done")
        gates_done, filled = sem("gates_done"), sem("filled")
        half_filled = sem("half_filled")
        p_bn, p_mv, p_ve, p_rstd, p_q = (sem(f"p_{s}") for s in ("bn", "mv", "ve", "rstd", "q"))
        p_qr, p_lo, qmask = sem("p_qr"), sem("p_lo"), sem("qmask")
        k_hi, k_done, v_done = sem("k_hi"), sem("k_done"), sem("v_done")
        s_mm, s_max, mrow_t, mrow_hi, mrow_sb = (
            sem(n) for n in ("s_mm", "s_max", "mrow_t", "mrow_hi", "mrow_sb"))
        st_mm, exp_done, av_mm, av_sb = sem("st_mm"), sem("exp_done"), sem("av_mm"), sem("av_sb")
        av_t, a_rec, a_norm, a_back = sem("av_t"), sem("a_rec"), sem("a_norm"), sem("a_back")
        x1_done, f_bn, f_mv, f_ve, f_rstd = (
            sem(n) for n in ("x1_done", "f_bn", "f_mv", "f_ve", "f_rstd"))
        h_done, h_t, hTh_done, hTl_done = sem("h_done"), sem("h_t"), sem("hTh_done"), sem("hTl_done")
        gu_mm, lg_done, nm_done, e8_done, th_done = (
            sem(n) for n in ("gu_mm", "lg_done", "nm_done", "e8_done", "th_done"))
        routed = sem("routed")
        w8_done = sem("w8_done")
        tmp_done, act_done, act_t, aTh_done, aTl_done = (
            sem(n) for n in ("tmp_done", "act_done", "act_t", "aTh_done", "aTl_done"))
        y_mm, y_done = sem("y_mm"), sem("y_done")

        block = ctx.enter_context(nc.Block())

        def steps(eng, step, before_experts=lambda: None):
            for par in range(2):
                step(Step(0, par, new=True, att=par == 1, ffn=False, prep=True))
            before_experts()
            with eng.Fori(1, B // 2) as r:
                for par in range(2):
                    step(Step(r, par, new=True, att=True, ffn=True, prep=True))
            for par in range(2):
                step(Step(B // 2, par, new=False, att=par == 0, ffn=True, prep=False))

        def stacked(src, b):
            return src[b].rearrange("(g p) l -> p g l", p=32)

        wgu_v = wgu.rearrange("(c p) n -> p c n", p=128)
        pieces = []
        for c in range(2):
            for a in range(0, 3 * STAGE, STAGE):
                z = a + STAGE
                pieces.append((wgu_v[:, c, a:z], wguh[:, c, a:z], wgul[:, c, a:z]))
        wd_v = wd.rearrange("(c p) n -> p c n", p=128)
        for a, z in ((0, 4), (4, 8), (8, 12), (12, NC)):
            pieces.append((wd_v[:, a:z, :], wdh[:, a:z, :], wdl[:, a:z, :]))
        NW = len(pieces)

        def staged(n):
            if n < 6:
                return wst[n % 2]
            chunks = pieces[n][1].shape[1]
            return wst[n % 2][:, 0:chunks * L].rearrange("p (c n) -> p c n", n=L)

        @block.sync
        def _(sp):
            def load_xy(lag, st, wrap):
                b, n = st.item(lag), st.buf(lag)
                src = b % B if wrap and not isinstance(b, int) else b
                if some(8 * (b - 1)):
                    sp.wait_ge(qmask, 8 * (b - 1))
                for j in range(PARTS):
                    sp.dma_start(xs[n][32 * j:32 * j + 32, :, :], stacked(x, src)).then_inc(x_in[n], 16)
                if some(2 * (b - 1)):
                    sp.wait_ge(k_done, 2 * (b - 1))
                for j in range(PARTS):
                    sp.dma_start(kr[n][32 * j:32 * j + 32, :, :], stacked(y, src)).then_inc(y_in[n], 16)

            load_xy(0, Step(0, 0, True, False, False, True), False)
            sp.dma_start(cst[:, :], consts).then_inc(const_in, 16)
            sp.dma_start(gates[:, 0:1], gx.partition_broadcast(128)).then_inc(const_in, 16)
            sp.dma_start(gates[:, 1:2], gf.partition_broadcast(128)).then_inc(const_in, 16)

            def step(st):
                b, f = st.item(0), st.item(2)
                if st.prep:
                    load_xy(-1, st, True)
                if st.new:
                    if some(b):
                        sp.wait_ge(v_done, b)
                    sp.dma_start(vraw[:, :, :], yT[b].rearrange("(c p) w -> p c w", p=128)).then_inc(v_in, 16)

                def mrow(hf):
                    sp.wait_ge(mrow_sb, 2 * b + hf + 1)
                    for n, part in enumerate((mh, ml)):
                        dst = qm[st.buf(0)][ROWS + n:ROWS + n + 1, 8 * hf:8 * hf + 8, :]
                        sp.dma_start(dst.rearrange("o h (c t) -> o (h c) t", t=128).bitcast(F32),
                                     part[:, hf, :].bitcast(F32)).then_inc(mrow_in[hf], 16)

                if st.new:
                    mrow(0)
                if st.ffn:
                    sp.wait_ge(y_done, f + 1)
                    sp.dma_start(out[f], yo[:, :]).then_inc(out_done, 16)
                if st.new:
                    mrow(1)
                if st.ffn and not (isinstance(f, int) and f + 1 == B):
                    sp.wait_ge(out_done, 16 * (f + 1))
                    sp.dma_start(xr[:, :], x[f + 1]).then_inc(xr_in, 16)

            def before_experts():
                sp.dma_start(xr[:, :], x[0]).then_inc(xr_in, 16)

            steps(sp, step, before_experts)
            sp.wait_ge(out_done, 16 * B)

        @block.gpsimd
        def _(pool):
            pool.memset(mhalf[:, :], -0.5).then_inc(half_filled, 1)
            pool.memset(zero[:, :], 0.0).then_inc(half_filled, 1)

            def copy(dst, src):
                p = src.start_partition()
                z = zero[p:p + src.shape[0], :]
                while len(z.shape) < len(src.shape):
                    z = z.unsqueeze(1)
                return pool.tensor_tensor(dst, src, z.to_broadcast(list(src.shape)), ALU.add)


            def rstd(lag, st, hf, last, count):
                n = 2 * st.item(lag) + hf
                pool.wait_ge(p_ve, n + 1)
                pool.wait_ge(last, count)
                pool.tensor_tensor(prs[:, hf, :], pve[:, hf, :], mhalf[0:ROWS, :], ALU.pow).then_inc(p_rstd, 1)

            def q_low(lag, st, hf, last, count):
                n = 2 * st.item(lag) + hf
                q = xs[st.buf(lag)][64:96, 2 * hf:2 * hf + 2, :]
                pool.wait_ge(p_q, 2 * n + 2)
                pool.wait_ge(last, count)
                copy(qr, q).then_inc(p_qr, 1)
                pool.wait_ge(p_qr, n + 1)
                pool.tensor_tensor(q, q, qr.bitcast(F32), ALU.subtract).then_inc(p_lo, 1)

            def k_parts(lag, st, hf, last, count):
                b, n = st.item(lag), st.buf(lag)
                pool.wait_ge(last, count)
                src = kr[n][:, 2 * hf:2 * hf + 2, :]
                dst = ks[n][:, 2 * hf:2 * hf + 2, :]
                if hf == 0:
                    pool.wait_ge(y_in[n], 48 * (st.uses(lag) + 1))
                if some(16 * (b - 2) + 8 * (hf + 1)):
                    pool.wait_ge(st_mm, 16 * (b - 2) + 8 * (hf + 1))
                copy(dst[0:ROWS], src).then_inc(k_hi, 1)
                pool.wait_ge(k_hi, 2 * b + hf + 1)
                pool.tensor_tensor(dst[32:64], src[32:64], dst[32:64].bitcast(F32),
                                   ALU.subtract).then_inc(k_done, 1)

            def values(st):
                b = st.item(0)
                pool.wait_ge(v_in, 16 * (b + 1))
                pool.wait_ge(k_done, 2 * b + 2)
                if some(4 * (b - 1)):
                    pool.wait_ge(av_mm, 4 * (b - 1))
                copy(vt[st.buf(0)][:, :, :, 0:CH],
                     vraw[:, :, :].rearrange("p c (h d) -> p c h d", d=CH)).then_inc(v_done, 1)

            def weights_low(n):
                _, hi, lo = pieces[n]
                pool.wait_ge(w_hi, n + 1)
                if some(n // 2):
                    pool.wait_ge(w_lo_pool, n // 2)
                pool.tensor_tensor(lo, staged(n), hi.bitcast(F32), ALU.subtract).then_inc(w_lo_pool, 1)

            pool.wait_ge(half_filled, 2)
            start = Step(0, -1, False, False, False, True)
            k_parts(-1, start, 0, half_filled, 2)
            rstd(-1, start, 0, k_done, 1)
            q_low(-1, start, 0, p_rstd, 1)

            def step(st):
                b = st.item(0)
                filling = st.new and not st.ffn
                if st.new:
                    rstd(0, st, 1, p_lo, 2 * b + 1)
                if st.ffn:
                    f = st.item(2)
                    pool.wait_ge(f_ve, f + 1)
                    if st.new:
                        pool.wait_ge(p_rstd, 2 * b + 2)
                    pool.tensor_tensor(frs[:, :], fve[:, :], mhalf[:, 0:1], ALU.pow).then_inc(f_rstd, 1)
                if st.new:
                    if st.ffn:
                        q_low(0, st, 1, f_rstd, st.item(2) + 1)
                    else:
                        q_low(0, st, 1, p_rstd, 2 * b + 2)
                    k_parts(0, st, 1, p_lo, 2 * b + 2)
                    values(st)
                    last, count = v_done, b + 1
                    if filling:
                        pool.wait_ge(last, count)
                        weights_low(1 + 4 * st.par)
                        last, count = w_lo_pool, 1 + 2 * st.par
                if st.prep:
                    k_parts(-1, st, 0, last, count)
                    rstd(-1, st, 0, k_done, 2 * b + 3)
                    q_low(-1, st, 0, p_rstd, 2 * b + 3)
                if filling:
                    pool.wait_ge(p_lo, 2 * b + 3)
                    for n in ((3,), (7, 9))[st.par]:
                        weights_low(n)
                    pool.wait_ge(w_lo_pool, 2 + 3 * st.par)

            steps(pool, step)

        @block.scalar
        def _(act):
            def masks(lag, st, hf, heads):
                b, n = st.item(lag), st.buf(lag)
                if heads[0] == 0:
                    act.wait_ge(p_lo, 2 * b + hf + 1)
                    if some(16 * (b - 2) + 8 * (hf + 1)):
                        act.wait_ge(st_mm, 16 * (b - 2) + 8 * (hf + 1))
                for i in heads:
                    dst = qm[n][0:ROWS, 8 * hf:8 * hf + 8, :].rearrange("p (g i) t -> p i g t", i=4)
                    act.activation(dst[:, i, :, :], xs[n][:, 2 * hf:2 * hf + 2, :], ACT.Copy,
                                   scale=cst[0:ROWS, C_MASK + i:C_MASK + i + 1]).then_inc(qmask, 1)

            def load_piece(n):
                if n >= 2:
                    act.wait_ge(w_lo_pool if n % 2 else w_lo_dve, n // 2)
                act.dma_start(staged(n), pieces[n][0]).then_inc(w_in[n % 2], 16)

            def round_piece(n):
                act.wait_ge(w_in[n % 2], 16 * (n // 2 + 1))
                act.activation(pieces[n][1], staged(n), ACT.Copy).then_inc(w_hi, 1)

            load_piece(0)
            load_piece(1)
            act.wait_ge(const_in, 48)
            act.activation(tg[:, :], gates[:, :], ACT.Tanh).then_inc(gates_done, 1)
            masks(-1, Step(0, -1, False, False, False, True), 0, range(4))

            def step(st):
                b, a, f = st.item(0), st.item(1), st.item(2)
                filling = st.new and not st.ffn
                for s in range(SLOTS):
                    if st.att:
                        act.wait_ge(st_mm, 16 * a + s + 1)
                        if s % 4 == 0:
                            if some(4 * a + s // 4 - 1):
                                act.wait_ge(av_mm, 4 * a + s // 4 - 1)
                        act.activation(probs[:, s % 8, :], ST[s % 2][:, :], ACT.Exp).then_inc(exp_done, 1)
                    if st.ffn:
                        if s == 4:
                            act.wait_ge(h_t, f + 1)
                            act.activation(hTh[:, :, :], M1[:, 0:L], ACT.Copy).then_inc(hTh_done, 1)
                        if s in (5, 7, 9, 11):
                            j = (s - 5) // 2
                            act.wait_ge(gu_mm, 8 * f + 2 * j + 1)
                            if j == 0:
                                act.activation(lg[:, :], GU[:, 0, FJ:FJ + EXPERTS], ACT.Copy).then_inc(lg_done, 1)
                            if j >= 2:
                                act.wait_ge(tmp_done, 4 * f + j - 1)
                            act.activation(th[:, j % 2, :], GU[:, 0, 0:FJ], ACT.Tanh,
                                           scale=0.5).then_inc(th_done, 1)
                            if j == 0:
                                act.wait_ge(nm_done, f + 1)
                                act.activation(e8[:, :], lg[:, :], ACT.Exp, bias=nm[:, 0:1],
                                               accum_out=es[:, :]).then_inc(e8_done, 1)
                        if s in (9, 11, 13, 14):
                            k = (9, 11, 13, 14).index(s)
                            n = min(4, NC - 4 * k)
                            act.wait_ge(act_t, 4 * f + k + 1)
                            act.activation(aTh[:, 4 * k:4 * k + n, :], M1[:, 0:128 * n],
                                           ACT.Copy).then_inc(aTh_done, 1)
                    if st.new and s in (5, 6, 7):
                        masks(0, st, 1, ((0,), (1, 2), (3,))[s - 5])
                    if st.prep and s in (13, 14, 15):
                        masks(-1, st, 0, ((0,), (1, 2), (3,))[s - 13])
                    if st.att and s in (9, 15):
                        k = s // 15
                        act.wait_ge(av_mm, 4 * a + 2 * k + 2)
                        if k == 0:
                            if some(2 * a):
                                act.wait_ge(av_t, 2 * a)
                        act.activation(avsb[:, 2 * k:2 * k + 2, :], AV[:, :], ACT.Copy).then_inc(av_sb, 1)
                    if filling and s in (2, 5, 8, 11, 14):
                        n = (2, 5, 8, 11, 14).index(s) + 5 * st.par
                        if n >= 1:
                            round_piece(n - 1)
                        if n >= 2:
                            load_piece(n)

            def before_experts():
                round_piece(NW - 1)
                act.wait_ge(w_lo_pool, NW // 2)

            steps(act, step, before_experts)

        @block.vector
        def _(dve):
            def stats(lag, st, hf):
                b, n = st.item(lag), st.buf(lag)
                m = 2 * b + hf
                if hf == 0:
                    dve.wait_ge(x_in[n], 48 * (st.uses(lag) + 1))
                for g in range(2):
                    dve.bn_stats(pst[:, hf, g, :], xs[n][:, 2 * hf + g, :]).then_inc(p_bn, 1)
                dve.wait_ge(p_bn, 2 * m + 2)
                dve.memset(unused[:, :], 0.0)
                for g in range(2):
                    dve.bn_aggr(pmv[:, hf, g, :], pst[:, hf, g, :]).then_inc(p_mv, 1)
                dve.wait_ge(p_mv, 2 * m + 2)
                dve.tensor_scalar(pve[:, hf, :], pmv[:, hf, :, 1], EPS, float(CH), ALU.add,
                                  ALU.mult).then_inc(p_ve, 1)

            def normal(lag, st, hf):
                b, n = st.item(lag), st.buf(lag)
                m = 2 * b + hf
                dve.wait_ge(p_rstd, m + 1)
                for g in range(2):
                    q = xs[n][:, 2 * hf + g, :]
                    dve.tensor_scalar(q, q, pmv[:, hf, g, 0:1], prs[:, hf, g:g + 1], ALU.subtract,
                                      ALU.mult).then_inc(p_q, 1)

            def mrow_parts(st, hf):
                n = 2 * st.item(0) + hf
                dve.wait_ge(mrow_t, n + 1)
                if some(32 * st.item(0)):
                    dve.wait_ge(mrow_in[hf], 32 * st.item(0))
                dve.tensor_copy(mh[:, hf, :], M1[0:SLOTS, 0:128]).then_inc(mrow_hi, 1)
                dve.wait_ge(mrow_hi, n + 1)
                dve.tensor_tensor(ml[:, hf, :], M1[0:SLOTS, 0:128], mh[:, hf, :].bitcast(F32),
                                  ALU.subtract).then_inc(mrow_sb, 1)

            def weights_low(n):
                _, hi, lo = pieces[n]
                dve.wait_ge(w_hi, n + 1)
                dve.tensor_tensor(lo, staged(n), hi.bitcast(F32), ALU.subtract).then_inc(w_lo_dve, 1)

            def attention_out(f):
                dve.wait_ge(av_t, 2 * f + 2)
                v = GU[:, :, :].rearrange("p c (h d) -> p c h d", d=VCOL)
                dve.reciprocal(rec[:, :, :], v[:, :, :, CH]).then_inc(a_rec, 1)
                dve.wait_ge(a_rec, f + 1)
                dve.tensor_tensor(aT[:, :, :, :], v[:, :, :, 0:CH],
                                  rec[:, :, :].unsqueeze(3).to_broadcast([128, 2, HEADS, CH]),
                                  ALU.mult).then_inc(a_norm, 1)

            def residual(f):
                dve.wait_ge(a_back, f + 1)
                dve.wait_ge(xr_in, 16 * (f + 1))
                dve.scalar_tensor_tensor(x1[:, :], M1[:, 0:L], tg[:, 0:1], xr[:, :], ALU.mult,
                                         ALU.add).then_inc(x1_done, 1)
                dve.wait_ge(x1_done, f + 1)
                dve.bn_stats(fst[:, :], x1[:, :]).then_inc(f_bn, 1)
                dve.wait_ge(f_bn, f + 1)
                dve.memset(unused[:, :], 0.0)
                dve.bn_aggr(fmv[:, :], fst[:, :]).then_inc(f_mv, 1)
                dve.wait_ge(f_mv, f + 1)
                dve.tensor_scalar(fve[:, :], fmv[:, 1:2], EPS, None, ALU.add).then_inc(f_ve, 1)

            def normal_h(f):
                dve.wait_ge(f_rstd, f + 1)
                dve.tensor_scalar(h[:, :], x1[:, :], fmv[:, 0:1], frs[:, 0:1], ALU.subtract,
                                  ALU.mult).then_inc(h_done, 1)

            def router(f):
                n = [0]

                def then(ins):
                    ins.then_inc(routed, 1)
                    n[0] += 1
                    dve.wait_ge(routed, 14 * f + n[0])

                dve.wait_ge(e8_done, f + 1)
                then(dve.reciprocal(er[:, :], es[:, :]))
                then(dve.tensor_scalar(sc[:, :], e8[:, :], er[:, 0:1], 0.5, ALU.mult, ALU.mult))
                then(dve.tensor_reduce(gs[:, :], sc[:, :].rearrange("p (g e) -> p g e", e=2), AX.X, ALU.max))

                def rank(v, size, cmp, lower, rk):
                    other = v.unsqueeze(1).to_broadcast([128, size, size])
                    own = v.unsqueeze(2).to_broadcast([128, size, size])
                    dve.tensor_tensor(cmp[:, 0], other, own, ALU.is_gt).then_inc(routed, 1)
                    n[0] += 1
                    then(dve.tensor_tensor(cmp[:, 1], other, own, ALU.is_equal))
                    then(dve.tensor_tensor(cmp[:, 2], cmp[:, 1], lower, ALU.mult))
                    then(dve.tensor_tensor(cmp[:, 1], cmp[:, 0], cmp[:, 2], ALU.add))
                    then(dve.tensor_reduce(rk, cmp[:, 1], AX.X, ALU.add))

                rank(gs[:, :], 4, cmp4, cst[:, C_L4:C_L4 + 16].rearrange("p (i j) -> p i j", j=4), rk4[:, :])
                dve.scalar_tensor_tensor(m8[:, :].rearrange("p (g e) -> p g e", e=2),
                                         rk4[:, :].unsqueeze(2).to_broadcast([128, 4, 2]), 2.0,
                                         sc[:, :].rearrange("p (g e) -> p g e", e=2),
                                         ALU.is_lt, ALU.mult).then_inc(routed, 1)
                n[0] += 1
                dve.wait_ge(routed, 14 * f + n[0])
                rank(m8[:, :], 8, cmp8, cst[:, C_L8:C_L8 + 64].rearrange("p (i j) -> p i j", j=8), rk8[:, :])
                assert n[0] == 14
                dve.scalar_tensor_tensor(w8[:, :], rk8[:, :], 2.0, m8[:, :], ALU.is_lt,
                                         ALU.mult).then_inc(w8_done, 1)

            def gate_block(f, j):
                dve.wait_ge(th_done, 4 * f + j + 1)
                if j:
                    dve.wait_ge(act_done, 4 * f + j)
                dve.scalar_tensor_tensor(tmp[:, :], th[:, j % 2, :], 1.0, GU[:, 0, 0:FJ], ALU.add,
                                         ALU.mult).then_inc(tmp_done, 1)

            def up_block(f, j):
                dve.wait_ge(gu_mm, 8 * f + 2 * j + 2)
                dve.wait_ge(tmp_done, 4 * f + j + 1)
                if j == 0:
                    dve.wait_ge(w8_done, f + 1)
                segments = expert_segments(j)
                for n, (c0, c1, e) in enumerate(segments):
                    ins = dve.scalar_tensor_tensor(
                        act_[:, j * FJ + c0:j * FJ + c1], tmp[:, c0:c1],
                        0.5 if e is None else w8[:, e:e + 1], GU[:, 1, c0:c1], ALU.mult, ALU.mult)
                    if n == len(segments) - 1:
                        ins.then_inc(act_done, 1)

            def act_low(f, k):
                n = min(4, NC - 4 * k)
                dve.wait_ge(aTh_done, 4 * f + k + 1)
                dve.tensor_tensor(aTl[:, 4 * k:4 * k + n, :], M1[:, 0:128 * n].rearrange("p (c t) -> p c t", t=128),
                                  aTh[:, 4 * k:4 * k + n, :].bitcast(F32), ALU.subtract).then_inc(aTl_done, 1)

            for n in range(2):
                dve.memset(ks[n][ROWS:KROWS, :, :].bitcast(F32), 1.0).then_inc(filled, 1)
            dve.memset(act_[:, F:FPAD], 0.0).then_inc(filled, 1)
            for n in range(2):
                dve.memset(vt[n][:, :, :, CH:VCOL], 0.0).then_inc(filled, 1)
            dve.wait_ge(filled, 5)
            for n in range(2):
                dve.memset(vt[n][:, :, :, CH:CH + 1], 1.0).then_inc(filled, 1)
            start = Step(0, -1, False, False, False, True)
            stats(-1, start, 0)
            normal(-1, start, 0)

            def step(st):
                b, f = st.item(0), st.item(2)
                filling = st.new and not st.ffn
                for s in range(SLOTS):
                    if st.new:
                        hf, r = divmod(s, 8)
                        if r == 0:
                            if some(2 * b + hf - 1):
                                dve.wait_ge(mrow_t, 2 * b + hf - 1)
                        dve.wait_ge(s_mm, 16 * b + s + 1)
                        dve.tensor_reduce(mx[:, hf, 2 * r:2 * r + 2], S[s % 2][:, :, :], AX.X, ALU.max,
                                          negate=True).then_inc(s_max, 1)
                        if s == 1:
                            stats(0, st, 1)
                        if s == 3:
                            normal(0, st, 1)
                        if s == 9:
                            mrow_parts(st, 0)
                    if st.prep:
                        if s == 8:
                            stats(-1, st, 0)
                        if s == 10:
                            normal(-1, st, 0)
                    if st.ffn:
                        if s == 0:
                            attention_out(f)
                        if s == 1:
                            residual(f)
                        if s == 2:
                            normal_h(f)
                        if s == 4:
                            dve.wait_ge(hTh_done, f + 1)
                            dve.tensor_tensor(hTl[:, :, :], M1[:, 0:L].rearrange("p (c t) -> p c t", t=W),
                                              hTh[:, :, :].bitcast(F32), ALU.subtract).then_inc(hTl_done, 1)
                        if s in (5, 7, 9, 11):
                            j = (s - 5) // 2
                            if j == 0:
                                dve.wait_ge(lg_done, f + 1)
                                dve.tensor_reduce(nm[:, :], lg[:, :], AX.X, ALU.max,
                                                  negate=True).then_inc(nm_done, 1)
                            gate_block(f, j)
                            if j == 0:
                                router(f)
                        if s in (6, 8, 10, 12):
                            up_block(f, (s - 6) // 2)
                        if s in (10, 12, 14, 15):
                            act_low(f, (10, 12, 14, 15).index(s))
                    if filling and s in ((8, 13), (4, 9, 14))[st.par]:
                        weights_low(4 + 2 * (s // 5) if st.par else 2 * (s // 10))
                if st.ffn:
                    dve.wait_ge(y_mm, f + 1)
                    dve.scalar_tensor_tensor(yo[:, :], GU[:, 0, 0:L], tg[:, 1:2], x1[:, :], ALU.mult,
                                             ALU.add).then_inc(y_done, 1)
                if st.new:
                    mrow_parts(st, 1)

            def before_experts():
                dve.wait_ge(gates_done, 1)
                dve.wait_ge(w_lo_pool, NW // 2)

            steps(dve, step, before_experts)

        @block.tensor
        def _(pe):
            def scores_n(st, s):
                b, n = st.item(0), st.buf(0)
                hf = s // 8
                if s % 8 == 0:
                    pe.wait_ge(qmask, 8 * b + 4 * (hf + 1))
                    pe.wait_ge(k_done, 2 * b + hf + 1)
                if some(16 * b + s - 1):
                    pe.wait_ge(s_max, 16 * b + s - 1)
                for tc in range(2):
                    mm = pe.matmul(S[s % 2][:, tc, :], qm[n][0:ROWS, s, 128 * tc:128 * tc + 128],
                                   ks[n][0:ROWS, s // 4, :], start=True, stop=True)
                mm.then_inc(s_mm, 1)

            def mrow_turn(st, hf):
                n = 2 * st.item(0) + hf
                pe.wait_ge(s_max, 8 * (n + 1))
                if hf == 0:
                    if some(n):
                        pe.wait_ge(mrow_sb, n)
                    if st.ffn:
                        pe.wait_ge(hTl_done, st.item(2) + 1)
                elif st.ffn:
                    pe.wait_ge(aTl_done, 4 * st.item(2) + 4)
                else:
                    pe.wait_ge(mrow_sb, n)
                pe.transpose(M1[0:SLOTS, 0:128], mx[:, hf, :], ident).then_inc(mrow_t, 1)

            def scores_a(st, s):
                a, n = st.item(1), st.buf(1)
                p, kc = divmod(s, 2)
                if s % 8 == 0:
                    pe.wait_ge(mrow_in[s // 8], 32 * (a + 1))
                if some(16 * a + s - 1):
                    pe.wait_ge(exp_done, 16 * a + s - 1)
                pe.matmul(ST[s % 2][:, :], ks[n][:, p // 2, 128 * kc:128 * kc + 128],
                          qm[n][:, 2 * p:2 * p + 2, :], start=True, stop=True).then_inc(st_mm, 1)

            def values(st, q):
                a, n = st.item(1), st.buf(1)
                pe.wait_ge(exp_done, 16 * a + 4 * q + 4)
                if q == 0:
                    pe.wait_ge(v_done, a + 1)
                if q % 2 == 0:
                    if some(2 * a + q // 2):
                        pe.wait_ge(av_sb, 2 * a + q // 2)
                for kc in range(2):
                    for i in range(4):
                        mm = pe.matmul(AV[32 * i:32 * i + 32, L * (q % 2):L * (q % 2) + L],
                                       vt[n][:, kc, 4 * q + i, :],
                                       probs[:, (4 * q + 2 * (i // 2) + kc) % 8, L * (i % 2):L * (i % 2) + L],
                                       start=(kc == 0), stop=(kc == 1))
                mm.then_inc(av_mm, 1)

            def gate_up(f, u):
                j, up = divmod(u, 2)
                if u == 0:
                    pe.wait_ge(hTl_done, f + 1)
                if j == 0:
                    pe.wait_ge(a_norm, f + 1)
                else:
                    pe.wait_ge(act_done if up else tmp_done, 4 * f + j)
                c0 = 2 * FJ * j + FJ * up + (EXPERTS if u else 0)
                width = FJ + (0 if u else EXPERTS)
                n = 0
                for kc in range(2):
                    for lhs, rhs in ((hTh, wguh), (hTh, wgul), (hTl, wguh)):
                        mm = pe.matmul(GU[:, up, 0:width], lhs[:, kc, :], rhs[:, kc, c0:c0 + width],
                                       start=(n == 0), stop=(n == 5))
                        n += 1
                mm.then_inc(gu_mm, 1)

            def act_turn(st, k):
                f = st.item(2)
                pe.wait_ge(act_done, 4 * f + (2, 3, 4, 4)[k])
                if k:
                    pe.wait_ge(aTl_done, 4 * f + k)
                elif st.new:
                    pe.wait_ge(mrow_sb, 2 * st.item(0) + 1)
                n = min(4, NC - 4 * k)
                for c in range(n):
                    mm = pe.transpose(M1[:, 128 * c:128 * c + 128], act_[:, 128 * (4 * k + c):128 * (4 * k + c) + 128],
                                      ident)
                mm.then_inc(act_t, 1)

            def down(f, c0, c1):
                pe.wait_ge(aTl_done, 4 * f + (c1 + 3) // 4)
                if c0 == 0:
                    pe.wait_ge(tmp_done, 4 * f + 4)
                for c in range(c0, c1):
                    K = min(128, F - 128 * c)
                    for n, (lhs, rhs) in enumerate(((aTh, wdh), (aTh, wdl), (aTl, wdh))):
                        mm = pe.matmul(GU[:, 0, 0:L], lhs[0:K, c, :], rhs[0:K, c, :],
                                       start=(c == 0 and n == 0), stop=(c == NC - 1 and n == 2))
                if c1 == NC:
                    mm.then_inc(y_mm, 1)

            pe.wait_ge(const_in, 48)
            pe.wait_ge(filled, 7)

            def step(st):
                b, f = st.item(0), st.item(2)
                for s in range(SLOTS):
                    if st.new:
                        scores_n(st, s)
                    if st.att:
                        scores_a(st, s)
                        if s in (4, 8, 12):
                            values(st, s // 4 - 1)
                    if st.new and s == 8:
                        mrow_turn(st, 0)
                    if st.ffn:
                        if s == 0:
                            pe.wait_ge(av_sb, 2 * f + 2)
                            if isinstance(b, int) and b > B:
                                pe.wait_ge(y_done, f)
                            else:
                                pe.wait_ge(mrow_sb, 2 * b)
                            for tc in range(2):
                                for q in range(GROUPS):
                                    mm = pe.transpose(GU[:, tc, 128 * q:128 * q + 128],
                                                      avsb[:, q, 128 * tc:128 * tc + 128], ident)
                                mm.then_inc(av_t, 1)
                        if s == 1:
                            pe.wait_ge(a_norm, f + 1)
                            for tc in range(2):
                                mm = pe.transpose(M1[:, 128 * tc:128 * tc + 128],
                                                  aT[:, tc, :, :].rearrange("p h d -> p (h d)"), ident)
                            mm.then_inc(a_back, 1)
                        if s == 3:
                            pe.wait_ge(h_done, f + 1)
                            for kc in range(2):
                                mm = pe.transpose(M1[:, 128 * kc:128 * kc + 128], h[:, 128 * kc:128 * kc + 128],
                                                  ident)
                            mm.then_inc(h_t, 1)
                        if s in (9, 11, 13, 14):
                            act_turn(st, (9, 11, 13, 14).index(s))
                        if 4 <= s < 12:
                            gate_up(f, s - 4)
                        if s == 12:
                            down(f, 0, 4)
                        if s == 13:
                            down(f, 4, 8)
                        if s == 15:
                            down(f, 8, 12)
                            down(f, 12, NC)
                    if st.att and s == 15:
                        values(st, 3)
                if st.new:
                    mrow_turn(st, 1)

            def before_experts():
                pe.wait_ge(w_lo_dve, NW // 2)
                pe.wait_ge(w_lo_pool, NW // 2)

            steps(pe, step, before_experts)


def constants():
    import numpy as np

    c = np.zeros((128, C_ALL), np.float32)
    c[:, C_ID:C_ID + 128] = np.eye(128)
    for i in range(4):
        c[:, C_MASK + i] = (np.arange(128) % 32) // CH == i
    c[:, C_L4:C_L4 + 16] = np.tril(np.ones((4, 4)), -1).reshape(1, 16)
    c[:, C_L8:C_L8 + 64] = np.tril(np.ones((8, 8)), -1).reshape(1, 64)
    return c


def kernel(x, ctx_2048, g_xattn, g_ffn, L0_ffn_gate_weight, L0_ffn_gate_w, L0_ffn_up_w, L0_ffn_down_w,
           L0_ffn_sh_gate_w, L0_ffn_sh_up_w, L0_ffn_sh_down_w):
    import numpy as np
    import concourse.bacc as bacc
    from concourse.bass_utils import run_bass_kernel_spmd

    a = np.asarray
    gate = np.concatenate([a(L0_ffn_sh_gate_w), a(L0_ffn_gate_w).reshape(-1, L)]).T
    up = np.concatenate([a(L0_ffn_sh_up_w), a(L0_ffn_up_w).reshape(-1, L)]).T
    cols = []
    for j in range(NJ):
        cols.append(gate[:, j * FJ:(j + 1) * FJ])
        if j == 0:
            cols.append(a(L0_ffn_gate_weight).T)
        cols.append(up[:, j * FJ:(j + 1) * FJ])
    wd = np.zeros((FPAD, L), np.float32)
    wd[0:FS] = a(L0_ffn_sh_down_w).T
    wd[FS:F] = a(L0_ffn_down_w).transpose(0, 2, 1).reshape(-1, L)
    arrays = {
        "x": a(x),
        "y": a(ctx_2048),
        "yT": np.ascontiguousarray(a(ctx_2048).transpose(0, 2, 1)),
        "gx": a(g_xattn),
        "gf": a(g_ffn),
        "wgu": np.ascontiguousarray(np.concatenate(cols, axis=1)),
        "wd": wd,
        "consts": constants(),
    }
    nc = bacc.Bacc("TRN2", target_bir_lowering=False, num_devices=1)
    args = [nc.dram_tensor(n, v.shape, mybir.dt.from_np(v.dtype), kind="ExternalInput").ap()
            for n, v in arrays.items()]
    out = nc.dram_tensor("out", (B, W, L), F32, kind="ExternalOutput").ap()
    flamingo_kernel(nc, *args, out)
    r = run_bass_kernel_spmd(nc, [arrays], core_ids=[0])
    return r.results[0]["out"]
```

```python
from contextlib import ExitStack

import concourse.bass as bass
from concourse import mybir

F32 = mybir.dt.float32
F32R = mybir.dt.float32r
ALU = mybir.AluOpType
ACT = mybir.ActivationFunctionType
AX = mybir.AxisListType

B, W, L = 8, 128, 256
HEADS, CH = 16, 8
GROUPS = 4
EXPERTS, FE, FS = 8, 176, 352
F = FS + EXPERTS * FE
BLOCKS = (FS, 470, 470, 468)
FIRST = (0, FS, FS + 470, FS + 940)
assert sum(BLOCKS) == F
NC = (F + 127) // 128
FPAD = NC * 128
EPS = 1e-5
PARTS = 3
ROWS = 32 * PARTS
KROWS = ROWS + 2
SLOTS = 16
VCOL = 32

C_ID, C_MASK, C_L4, C_L8 = 0, 128, 132, 148
C_ALL = 212


def expert_segments(j):
    edges = [0] + [FS + e * FE for e in range(EXPERTS + 1)]
    out = []
    for n in range(EXPERTS + 1):
        a, b = max(edges[n], FIRST[j]), min(edges[n + 1], FIRST[j] + BLOCKS[j])
        if a < b:
            out.append((a - FIRST[j], b - FIRST[j], n - 1 if n else None))
    return out


def gate_up_columns(j, up):
    if (j, up) == (0, 0):
        return 0, BLOCKS[0] + EXPERTS
    return EXPERTS + 2 * FIRST[j] + up * BLOCKS[j], BLOCKS[j]


def some(count):
    return not isinstance(count, int) or count > 0


class Step:

    def __init__(self, r, par, prep=True, new=True, att=True, comb=True, ffn=True, filling=None):
        self.r, self.par = r, par
        self.prep, self.new, self.att, self.comb, self.ffn = prep, new, att, comb, ffn
        self.filling = filling

    def item(self, lag):
        return 2 * self.r + (self.par - lag)

    def buf(self, lag):
        return (self.par - lag) % 2

    def uses(self, lag):
        return self.r + (self.par - lag) // 2


def flamingo_kernel(nc, x, y, yT, gx, gf, wgu, wd, consts, out):
    with ExitStack() as ctx:
        def sb(name, shape, dt=F32):
            return ctx.enter_context(nc.sbuf_tensor(name, shape, dt))

        def ps(name, shape):
            return ctx.enter_context(nc.psum_tensor(name, shape, F32))

        def sem(name):
            return ctx.enter_context(nc.semaphore(name))

        cst = sb("cst", [128, C_ALL])
        ident = cst[:, C_ID:C_ID + 128]
        wguh = sb("wguh", [128, 2, 2 * F + EXPERTS], F32R)
        wgul = sb("wgul", [128, 2, 2 * F + EXPERTS], F32R)
        wdh = sb("wdh", [128, NC, L], F32R)
        wdl = sb("wdl", [128, NC, L], F32R)
        gates = sb("gates", [128, 2])
        tg = sb("tg", [128, 2])
        xs = [sb(f"xs{n}", [ROWS, GROUPS, L]) for n in range(2)]
        kr = [sb(f"kr{n}", [ROWS, GROUPS, L]) for n in range(2)]
        parts = sb("parts", [ROWS, 2, L], F32R)
        qr = parts[64:96, :, :]
        mh, ml = (parts[0:SLOTS, n, :].rearrange("p (c t) -> p c t", t=128) for n in range(2))
        qm = [sb(f"qm{n}", [KROWS, HEADS, L], F32R) for n in range(2)]
        ks = [sb(f"ks{n}", [KROWS, GROUPS, L], F32R) for n in range(2)]
        vraw = sb("vraw", [128, 2, W])
        vt = [sb(f"vt{n}", [128, 2, HEADS, VCOL]) for n in range(2)]
        pst = sb("pst", [ROWS, 2, 2, 6])
        pmv = sb("pmv", [ROWS, 2, 2, 2])
        pve = sb("pve", [ROWS, 2, 2])
        prs = sb("prs", [ROWS, 2, 2])
        mhalf = sb("mhalf", [128, 2])
        zero = sb("zero", [128, 1])
        unused = sb("unused", [1, 1])
        mx = sb("mx", [128, 2, SLOTS])
        probs = sb("probs", [128, 8, 512])
        avsb = sb("avsb", [128, GROUPS, L])
        rec = sb("rec", [128, 2, HEADS])
        aT = sb("aT", [128, 2, HEADS, CH])
        xr = sb("xr", [128, L])
        x1 = [sb(f"x1{n}", [128, L]) for n in range(2)]
        h = sb("h", [128, L])
        fst = sb("fst", [128, 6])
        fmv = sb("fmv", [128, 2])
        fve = sb("fve", [128, 1])
        frs = sb("frs", [128, 1])
        hTh = sb("hTh", [128, 2, W], F32R)
        hTl = sb("hTl", [128, 2, W], F32R)
        lg = sb("lg", [128, EXPERTS])
        nm = sb("nm", [128, 1])
        e8 = sb("e8", [128, EXPERTS])
        es = sb("es", [128, 1])
        er = sb("er", [128, 1])
        sc = sb("sc", [128, EXPERTS])
        gs = sb("gs", [128, 4])
        cmp4 = sb("cmp4", [128, 4, 2 * 4])
        rk4 = sb("rk4", [128, 4])
        m8 = sb("m8", [128, EXPERTS])
        cmp8 = sb("cmp8", [128, 8, 2 * 8])
        rk8 = sb("rk8", [128, EXPERTS])
        w8 = sb("w8", [128, EXPERTS])
        thy = sb("thy", [128, 2 * max(BLOCKS) + L])
        th = thy[:, 0:2 * max(BLOCKS)].rearrange("p (n c) -> p n c", n=2)
        yo = thy[:, 2 * max(BLOCKS):]
        tmp = sb("tmp", [128, max(BLOCKS)])
        act_ = sb("act_", [128, 4 * max(BLOCKS)])
        aTh = sb("aTh", [128, NC, W], F32R)
        aTl = sb("aTl", [128, NC, W], F32R)

        wst = [thy[:, 0:2 * max(BLOCKS)], act_[:, 0:2 * max(BLOCKS)], act_[:, 2 * max(BLOCKS):]]

        S = [ps(f"S{n}", [128, 2, L]) for n in range(2)]
        ST = [ps(f"ST{n}", [128, 512]) for n in range(2)]
        GU = ps("GU", [128, 2, 512])
        AV = ps("AV", [128, 512])
        M1 = ps("M1", [128, 512])
        G = GU[:, 0, :]

        const_in, gates_in = sem("const_in"), sem("gates_in")
        w_in = [sem(f"w_in{n}") for n in range(3)]
        w_hi, w_lo = sem("w_hi"), sem("w_lo")
        x_in = [sem(f"x_in{n}") for n in range(2)]
        y_in = [sem(f"y_in{n}") for n in range(2)]
        mrow_in = [sem(f"mrow_in{n}") for n in range(2)]
        v_in, xr_in, out_done = sem("v_in"), sem("xr_in"), sem("out_done")
        gates_done, filled = sem("gates_done"), sem("filled")
        pool_filled = sem("pool_filled")
        p_bn, p_mv, p_ve, p_rstd, p_mid, p_q = (
            sem(f"p_{s}") for s in ("bn", "mv", "ve", "rstd", "mid", "q"))
        p_qr, p_lo, qmask = sem("p_qr"), sem("p_lo"), sem("qmask")
        k_hi, k_done, v_done = sem("k_hi"), sem("k_done"), sem("v_done")
        s_mm, s_max, mrow_t, mrow_hi, mrow_sb = (
            sem(n) for n in ("s_mm", "s_max", "mrow_t", "mrow_hi", "mrow_sb"))
        st_mm, exp_done, av_mm, av_sb = sem("st_mm"), sem("exp_done"), sem("av_mm"), sem("av_sb")
        av_t, a_rec, a_norm, a_back = sem("av_t"), sem("a_rec"), sem("a_norm"), sem("a_back")
        x1_done, f_bn, f_mv, f_ve, f_rstd = (
            sem(n) for n in ("x1_done", "f_bn", "f_mv", "f_ve", "f_rstd"))
        h_done, h_t, hTh_done, hTl_done = sem("h_done"), sem("h_t"), sem("hTh_done"), sem("hTl_done")
        gu_mm, lg_done, nm_done, e8_done, th_done = (
            sem(n) for n in ("gu_mm", "lg_done", "nm_done", "e8_done", "th_done"))
        routed = sem("routed")
        w8_done = sem("w8_done")
        tmp_done, act_done, act_t, aTh_done, aTl_done = (
            sem(n) for n in ("tmp_done", "act_done", "act_t", "aTh_done", "aTl_done"))
        y_mm, y_done = sem("y_mm"), sem("y_done")

        block = ctx.enter_context(nc.Block())

        def steps(eng, step):
            step(Step(0, 0, att=False, comb=False, ffn=False, filling=0))
            step(Step(0, 1, comb=False, ffn=False, filling=1))
            step(Step(1, 0, ffn=False, filling=2))
            step(Step(1, 1))
            with eng.Fori(2, B // 2) as r:
                for par in range(2):
                    step(Step(r, par))
            step(Step(B // 2, 0, prep=False, new=False))
            step(Step(B // 2, 1, prep=False, new=False, att=False))
            step(Step(B // 2 + 1, 0, prep=False, new=False, att=False, comb=False))

        def stacked(src, b):
            return src[b].rearrange("(g p) l -> p g l", p=32)

        wgu_v = wgu.rearrange("(c p) n -> p c n", p=128)
        pieces = []
        for u in range(8):
            a, width = gate_up_columns(*divmod(u, 2))
            pieces.append((wgu_v[:, :, a:a + width], wguh[:, :, a:a + width], wgul[:, :, a:a + width]))
        wd_v = wd.rearrange("(c p) n -> p c n", p=128)
        for a in range(0, NC, 3):
            z = min(a + 3, NC)
            pieces.append((wd_v[:, a:z, :], wdh[:, a:z, :], wdl[:, a:z, :]))
        NW = len(pieces)

        def staged(n):
            c, width = pieces[n][1].shape[1:]
            return wst[n % 3][:, 0:c * width].rearrange("p (c n) -> p c n", n=width)

        rounded_at = ((0, 7), (0, 11), (0, 15), (1, 1), (1, 5), (1, 7), (1, 11), (1, 14),
                      (2, 1), (2, 4), (2, 7), (2, 11), (2, 13))
        low_at = ((0, 8), (0, 12), (1, 1), (1, 3), (1, 6), (1, 8), (1, 12), (1, 15),
                  (2, 3), (2, 5), (2, 8), (2, 12), (2, 14))

        turned = (M1, M1, G, M1)
        rows_turned = (G[0:SLOTS, L:L + 128], M1[0:SLOTS, 0:128])

        @block.sync
        def _(sp):
            def load_x(n, src):
                for j in range(PARTS):
                    sp.dma_start(xs[n][32 * j:32 * j + 32, :, :], stacked(x, src)).then_inc(x_in[n], 16)

            def load_y(n, src):
                for j in range(PARTS):
                    sp.dma_start(kr[n][32 * j:32 * j + 32, :, :], stacked(y, src)).then_inc(y_in[n], 16)

            def load_v(src):
                sp.dma_start(vraw[:, :, :], yT[src].rearrange("(c p) w -> p c w", p=128)).then_inc(v_in, 16)

            load_x(0, 0)
            sp.dma_start(cst[:, :], consts).then_inc(const_in, 16)
            load_y(0, 0)
            sp.dma_start(gates[:, 0:1], gx.partition_broadcast(128)).then_inc(gates_in, 16)
            sp.dma_start(gates[:, 1:2], gf.partition_broadcast(128)).then_inc(gates_in, 16)
            load_v(0)
            load_x(1, 1)
            load_y(1, 1)
            for n in range(3):
                sp.dma_start(staged(n), pieces[n][0]).then_inc(w_in[n], 16)

            def mrow(b, n, hf):
                sp.wait_ge(mrow_sb, 2 * b + hf + 1)
                for row, part in enumerate((mh, ml)):
                    dst = qm[n][ROWS + row:ROWS + row + 1, 8 * hf:8 * hf + 8, :]
                    sp.dma_start(dst.rearrange("o h (c t) -> o (h c) t", t=128).bitcast(F32),
                                 part[:, hf, :].bitcast(F32)).then_inc(mrow_in[hf], 16)

            def step(st):
                b, a, c, g = (st.item(lag) for lag in range(4))
                if st.comb:
                    if some(c):
                        sp.wait_ge(x1_done, c)
                    sp.dma_start(xr[:, :], x[c]).then_inc(xr_in, 16)
                if st.att:
                    mrow(a, st.buf(1), 1)
                if st.new:
                    sp.wait_ge(v_done, b + 1)
                    load_v((b + 1) % B)
                    sp.wait_ge(qmask, 8 * (b + 1))
                    load_x(st.buf(0), (b + 2) % B)
                    sp.wait_ge(k_done, 2 * (b + 1))
                    load_y(st.buf(0), (b + 2) % B)
                    mrow(b, st.buf(0), 0)
                if st.ffn:
                    sp.wait_ge(y_done, g + 1)
                    sp.dma_start(out[g], yo).then_inc(out_done, 16)

            steps(sp, step)
            sp.wait_ge(out_done, 16 * B)

        @block.gpsimd
        def _(pool):
            pool.memset(mhalf[:, :], -0.5).then_inc(pool_filled, 1)
            pool.memset(zero[:, :], 0.0).then_inc(pool_filled, 1)
            for n in range(2):
                pool.memset(vt[n][:, :, :, CH + 1:VCOL], 0.0).then_inc(pool_filled, 1)
                pool.memset(vt[n][:, :, :, CH:CH + 1], 1.0).then_inc(pool_filled, 1)

            def copy(dst, src):
                p = src.start_partition()
                z = zero[p:p + src.shape[0], :]
                while len(z.shape) < len(src.shape):
                    z = z.unsqueeze(1)
                return pool.tensor_tensor(dst, src, z.to_broadcast(list(src.shape)), ALU.add)


            def rstd(lag, st, hf, last, count):
                n = 2 * st.item(lag) + hf
                pool.wait_ge(p_ve, n + 1)
                pool.wait_ge(last, count)
                pool.tensor_tensor(prs[:, hf, :], pve[:, hf, :], mhalf[0:ROWS, :], ALU.pow).then_inc(p_rstd, 1)

            def normal(lag, st, hf):
                n = 2 * st.item(lag) + hf
                q = xs[st.buf(lag)][:, 2 * hf:2 * hf + 2, :]
                pool.wait_ge(p_rstd, n + 1)
                pool.tensor_tensor(q, q, pmv[:, hf, :, 0:1].to_broadcast([ROWS, 2, L]),
                                   ALU.subtract).then_inc(p_mid, 1)
                pool.wait_ge(p_mid, n)
                pool.tensor_tensor(q, q, prs[:, hf, :].unsqueeze(2).to_broadcast([ROWS, 2, L]),
                                   ALU.mult).then_inc(p_q, 1)

            def q_low(lag, st, hf):
                n = 2 * st.item(lag) + hf
                q = xs[st.buf(lag)][64:96, 2 * hf:2 * hf + 2, :]
                pool.wait_ge(p_q, n + 1)
                copy(qr, q).then_inc(p_qr, 1)
                pool.wait_ge(p_qr, n + 1)
                pool.tensor_tensor(q, q, qr.bitcast(F32), ALU.subtract).then_inc(p_lo, 1)

            def k_parts(lag, st, hf, last, count):
                b, n = st.item(lag), st.buf(lag)
                pool.wait_ge(last, count)
                src = kr[n][:, 2 * hf:2 * hf + 2, :]
                dst = ks[n][:, 2 * hf:2 * hf + 2, :]
                if hf == 0:
                    pool.wait_ge(y_in[n], 48 * (st.uses(lag) + 1))
                if some(16 * (b - 2) + 8 * (hf + 1)):
                    pool.wait_ge(st_mm, 16 * (b - 2) + 8 * (hf + 1))
                copy(dst[0:ROWS], src).then_inc(k_hi, 1)
                pool.wait_ge(k_hi, 2 * b + hf + 1)
                pool.tensor_tensor(dst[32:64], src[32:64], dst[32:64].bitcast(F32),
                                   ALU.subtract).then_inc(k_done, 1)

            def values(st):
                b = st.item(0)
                pool.wait_ge(v_in, 16 * (b + 1))
                pool.wait_ge(k_done, 2 * b + 2)
                if some(4 * (b - 1)):
                    pool.wait_ge(av_mm, 4 * (b - 1))
                copy(vt[st.buf(0)][:, :, :, 0:CH],
                     vraw[:, :, :].rearrange("p c (h d) -> p c h d", d=CH)).then_inc(v_done, 1)

            pool.wait_ge(pool_filled, 6)
            start = Step(0, -1)
            rstd(-1, start, 0, pool_filled, 6)
            rstd(-1, start, 1, p_rstd, 1)
            pool.wait_ge(p_lo, 1)
            normal(-1, start, 1)
            q_low(-1, start, 1)

            def step(st):
                b, c = st.item(0), st.item(2)
                if st.new:
                    k_parts(0, st, 1, p_lo, 2 * b + 2)
                    values(st)
                if st.prep:
                    rstd(-1, st, 0, v_done, b + 1)
                    normal(-1, st, 0)
                    q_low(-1, st, 0)
                    k_parts(-1, st, 0, p_lo, 2 * b + 3)
                if st.comb:
                    pool.wait_ge(f_ve, c + 1)
                    if st.prep:
                        pool.wait_ge(k_done, 2 * b + 3)
                    else:
                        pool.wait_ge(p_lo, 2 * (B + 1))
                    pool.tensor_tensor(frs[:, :], fve[:, :], mhalf[:, 0:1], ALU.pow).then_inc(f_rstd, 1)
                    pool.wait_ge(f_rstd, c + 1)
                if st.prep:
                    rstd(-1, st, 1, *((f_rstd, c + 1) if st.comb else (k_done, 2 * b + 3)))
                    normal(-1, st, 1)
                    q_low(-1, st, 1)

            steps(pool, step)

        @block.scalar
        def _(act):
            def masks(lag, st, hf, i):
                b, n = st.item(lag), st.buf(lag)
                if i == 0:
                    act.wait_ge(p_lo, 2 * b + hf + 1)
                    if some(16 * (b - 2) + 8 * (hf + 1)):
                        act.wait_ge(st_mm, 16 * (b - 2) + 8 * (hf + 1))
                dst = qm[n][0:ROWS, 8 * hf:8 * hf + 8, :].rearrange("p (g i) t -> p i g t", i=4)
                act.activation(dst[:, i, :, :], xs[n][:, 2 * hf:2 * hf + 2, :], ACT.Copy,
                               scale=cst[0:ROWS, C_MASK + i:C_MASK + i + 1]).then_inc(qmask, 1)

            def round_piece(n):
                act.wait_ge(w_in[n % 3], 16 * (n // 3 + 1))
                act.activation(pieces[n][1], staged(n), ACT.Copy).then_inc(w_hi, 1)
                if 1 <= n < NW - 2:
                    act.wait_ge(w_lo, n)
                    act.dma_start(staged(n + 2), pieces[n + 2][0]).then_inc(w_in[(n + 2) % 3], 16)

            act.wait_ge(const_in, 16)
            for i in range(4):
                masks(-1, Step(0, -1), 0, i)
            act.wait_ge(gates_in, 32)
            act.activation(tg[:, :], gates[:, :], ACT.Tanh).then_inc(gates_done, 1)

            def tanh_block(g, j):
                act.wait_ge(gu_mm, 8 * g + 2 * j + 1)
                if j == 0:
                    act.activation(lg[:, :], GU[:, 0, FS:FS + EXPERTS], ACT.Copy).then_inc(lg_done, 1)
                if j >= 2:
                    act.wait_ge(tmp_done, 4 * g + j - 1)
                act.activation(th[:, j % 2, 0:BLOCKS[j]], GU[:, 0, 0:BLOCKS[j]], ACT.Tanh,
                               scale=0.5).then_inc(th_done, 1)
                if j == 0:
                    act.wait_ge(nm_done, g + 1)
                    act.activation(e8[:, :], lg[:, :], ACT.Exp, bias=nm[:, 0:1],
                                   accum_out=es[:, :]).then_inc(e8_done, 1)

            def act_high(g, k):
                n = min(4, NC - 4 * k)
                act.wait_ge(act_t, 4 * g + k + 1)
                act.activation(aTh[:, 4 * k:4 * k + n, :], turned[k][:, 0:128 * n], ACT.Copy).then_inc(aTh_done, 1)

            def attention_copy(a, k):
                act.wait_ge(av_mm, 4 * a + 2 * k + 2)
                if k == 0 and some(2 * a):
                    act.wait_ge(av_t, 2 * a)
                act.activation(avsb[:, 2 * k:2 * k + 2, :], AV[:, :], ACT.Copy).then_inc(av_sb, 1)

            def step(st):
                b, a, c, g = (st.item(lag) for lag in range(4))
                if st.ffn and not some(g):
                    act.wait_ge(w_lo, NW)
                for s in range(SLOTS):
                    if st.comb:
                        if s == 2:
                            attention_copy(c, 1)
                        if s == 14:
                            act.wait_ge(h_t, c + 1)
                            act.activation(hTh[:, :, :], G[:, 0:L], ACT.Copy).then_inc(hTh_done, 1)
                    if st.att and s == 10:
                        attention_copy(a, 0)
                    if st.ffn and s in (8, 11, 12, 13):
                        act_high(g, (8, 11, 12, 13).index(s))
                    if st.att:
                        act.wait_ge(st_mm, 16 * a + s + 1)
                        if s % 4 == 0 and some(4 * a + s // 4 - 1):
                            act.wait_ge(av_mm, 4 * a + s // 4 - 1)
                        act.activation(probs[:, s % 8, :], ST[s % 2][:, :], ACT.Exp).then_inc(exp_done, 1)
                    if st.ffn and s in (0, 2, 5, 7):
                        tanh_block(g, (0, 2, 5, 7).index(s))
                    if st.new and s in (3, 4, 5, 6):
                        masks(0, st, 1, s - 3)
                    if st.prep and s in (9, 10, 14, 15):
                        masks(-1, st, 0, (9, 10, 14, 15).index(s))
                    if (st.filling, s) in rounded_at:
                        round_piece(rounded_at.index((st.filling, s)))

            steps(act, step)

        @block.vector
        def _(dve):
            def stats(lag, st, hf):
                b, n = st.item(lag), st.buf(lag)
                m = 2 * b + hf
                if hf == 0:
                    dve.wait_ge(x_in[n], 48 * (st.uses(lag) + 1))
                for g in range(2):
                    dve.bn_stats(pst[:, hf, g, :], xs[n][:, 2 * hf + g, :]).then_inc(p_bn, 1)
                dve.wait_ge(p_bn, 2 * m + 2)
                dve.memset(unused[:, :], 0.0)
                for g in range(2):
                    dve.bn_aggr(pmv[:, hf, g, :], pst[:, hf, g, :]).then_inc(p_mv, 1)
                dve.wait_ge(p_mv, 2 * m + 2)
                dve.tensor_scalar(pve[:, hf, :], pmv[:, hf, :, 1], EPS, float(CH), ALU.add,
                                  ALU.mult).then_inc(p_ve, 1)

            def first_half():
                k, dst = kr[0][:, 0:2, :], ks[0][:, 0:2, :]
                dve.wait_ge(y_in[0], 48)
                dve.tensor_copy(dst[0:ROWS], k).then_inc(k_hi, 1)
                dve.wait_ge(k_hi, 1)
                dve.tensor_tensor(dst[32:64], k[32:64], dst[32:64].bitcast(F32), ALU.subtract).then_inc(k_done, 1)
                dve.wait_ge(p_rstd, 1)
                for g in range(2):
                    q = xs[0][:, g, :]
                    ins = dve.tensor_scalar(q, q, pmv[:, 0, g, 0:1], prs[:, 0, g:g + 1], ALU.subtract, ALU.mult)
                ins.then_inc(p_q, 1)
                dve.wait_ge(p_q, 1)
                q = xs[0][64:96, 0:2, :]
                dve.tensor_copy(qr, q).then_inc(p_qr, 1)
                dve.wait_ge(p_qr, 1)
                dve.tensor_tensor(q, q, qr.bitcast(F32), ALU.subtract).then_inc(p_lo, 1)

            def mrow_parts(b, hf):
                n = 2 * b + hf
                dve.wait_ge(mrow_t, n + 1)
                if some(32 * b):
                    dve.wait_ge(mrow_in[hf], 32 * b)
                dve.tensor_copy(mh[:, hf, :], rows_turned[hf]).then_inc(mrow_hi, 1)
                dve.wait_ge(mrow_hi, n + 1)
                dve.tensor_tensor(ml[:, hf, :], rows_turned[hf], mh[:, hf, :].bitcast(F32),
                                  ALU.subtract).then_inc(mrow_sb, 1)

            def weights_low(n):
                _, hi, lo = pieces[n]
                dve.wait_ge(w_hi, n + 1)
                dve.tensor_tensor(lo, staged(n), hi.bitcast(F32), ALU.subtract).then_inc(w_lo, 1)

            def attention_out(c, tc):
                dve.wait_ge(av_t, 2 * c + tc + 1)
                v = M1[:, :].rearrange("p (h d) -> p h d", d=VCOL)
                dve.reciprocal(rec[:, tc, :], v[:, :, CH]).then_inc(a_rec, 1)
                dve.wait_ge(a_rec, 2 * c + tc + 1)
                dve.tensor_tensor(aT[:, tc, :, :], v[:, :, 0:CH],
                                  rec[:, tc, :].unsqueeze(2).to_broadcast([128, HEADS, CH]),
                                  ALU.mult).then_inc(a_norm, 1)

            def residual(c, x1c):
                dve.wait_ge(a_back, c + 1)
                dve.wait_ge(xr_in, 16 * (c + 1))
                dve.scalar_tensor_tensor(x1c[:, :], G[:, 0:L], tg[:, 0:1], xr[:, :], ALU.mult,
                                         ALU.add).then_inc(x1_done, 1)

            def residual_stats(c, x1c):
                dve.wait_ge(x1_done, c + 1)
                dve.bn_stats(fst[:, :], x1c[:, :]).then_inc(f_bn, 1)
                dve.wait_ge(f_bn, c + 1)
                dve.memset(unused[:, :], 0.0)
                dve.bn_aggr(fmv[:, :], fst[:, :]).then_inc(f_mv, 1)
                dve.wait_ge(f_mv, c + 1)
                dve.tensor_scalar(fve[:, :], fmv[:, 1:2], EPS, None, ALU.add).then_inc(f_ve, 1)

            def normal_h(c, x1c):
                dve.wait_ge(f_rstd, c + 1)
                dve.tensor_scalar(h[:, :], x1c[:, :], fmv[:, 0:1], frs[:, 0:1], ALU.subtract,
                                  ALU.mult).then_inc(h_done, 1)

            def h_low(c):
                dve.wait_ge(hTh_done, c + 1)
                dve.tensor_tensor(hTl[:, :, :], G[:, 0:L].rearrange("p (c t) -> p c t", t=W),
                                  hTh[:, :, :].bitcast(F32), ALU.subtract).then_inc(hTl_done, 1)

            ROUTED = 12

            def router_scores(f):
                dve.wait_ge(e8_done, f + 1)
                dve.reciprocal(er[:, :], es[:, :]).then_inc(routed, 1)
                dve.wait_ge(routed, ROUTED * f + 1)
                dve.tensor_scalar(sc[:, :], e8[:, :], er[:, 0:1], 0.5, ALU.mult, ALU.mult).then_inc(routed, 1)
                dve.wait_ge(routed, ROUTED * f + 2)
                dve.tensor_reduce(gs[:, :], sc[:, :].rearrange("p (g e) -> p g e", e=2), AX.X,
                                  ALU.max).then_inc(routed, 1)

            def compare(f, done, v, size, cmp):
                other = v.unsqueeze(1).to_broadcast([128, size, size])
                own = v.unsqueeze(2).to_broadcast([128, size, size])
                dve.wait_ge(routed, ROUTED * f + done)
                dve.tensor_tensor(cmp[:, :, 0:size], other, own, ALU.is_gt).then_inc(routed, 1)
                dve.tensor_tensor(cmp[:, :, size:2 * size], other, own, ALU.is_equal).then_inc(routed, 1)

            def rank(f, done, size, cmp, lower, rk):
                dve.wait_ge(routed, ROUTED * f + done)
                dve.tensor_tensor(cmp[:, :, size:2 * size], cmp[:, :, size:2 * size],
                                  lower.rearrange("p (i j) -> p i j", j=size), ALU.mult).then_inc(routed, 1)
                dve.wait_ge(routed, ROUTED * f + done + 1)
                dve.tensor_reduce(rk, cmp[:, :, :], AX.X, ALU.add).then_inc(routed, 1)

            def keep_groups(f):
                dve.wait_ge(routed, ROUTED * f + 7)
                dve.scalar_tensor_tensor(m8[:, :].rearrange("p (g e) -> p g e", e=2),
                                         rk4[:, :].unsqueeze(2).to_broadcast([128, 4, 2]), 2.0,
                                         sc[:, :].rearrange("p (g e) -> p g e", e=2),
                                         ALU.is_lt, ALU.mult).then_inc(routed, 1)

            def keep_experts(f):
                dve.wait_ge(routed, ROUTED * f + 12)
                dve.scalar_tensor_tensor(w8[:, :], rk8[:, :], 2.0, m8[:, :], ALU.is_lt,
                                         ALU.mult).then_inc(w8_done, 1)

            def gate_block(f, j):
                if j == 0:
                    dve.wait_ge(lg_done, f + 1)
                    dve.tensor_reduce(nm[:, :], lg[:, :], AX.X, ALU.max, negate=True).then_inc(nm_done, 1)
                dve.wait_ge(th_done, 4 * f + j + 1)
                if j:
                    dve.wait_ge(act_done, 4 * f + j)
                dve.scalar_tensor_tensor(tmp[:, 0:BLOCKS[j]], th[:, j % 2, 0:BLOCKS[j]], 1.0,
                                         GU[:, 0, 0:BLOCKS[j]], ALU.add, ALU.mult).then_inc(tmp_done, 1)

            def up_block(f, j):
                dve.wait_ge(gu_mm, 8 * f + 2 * j + 2)
                dve.wait_ge(tmp_done, 4 * f + j + 1)
                if j == 1:
                    dve.wait_ge(w8_done, f + 1)
                segments = expert_segments(j)
                for n, (c0, c1, e) in enumerate(segments):
                    ins = dve.scalar_tensor_tensor(
                        act_[:, FIRST[j] + c0:FIRST[j] + c1], tmp[:, c0:c1],
                        0.5 if e is None else w8[:, e:e + 1], GU[:, 1, c0:c1], ALU.mult, ALU.mult)
                    if n == len(segments) - 1:
                        ins.then_inc(act_done, 1)

            def act_low(f, k):
                n = min(4, NC - 4 * k)
                dve.wait_ge(aTh_done, 4 * f + k + 1)
                dve.tensor_tensor(aTl[:, 4 * k:4 * k + n, :], turned[k][:, 0:128 * n].rearrange("p (c t) -> p c t", t=128),
                                  aTh[:, 4 * k:4 * k + n, :].bitcast(F32), ALU.subtract).then_inc(aTl_done, 1)

            for n in range(2):
                dve.memset(ks[n][ROWS:KROWS, :, :].bitcast(F32), 1.0).then_inc(filled, 1)
            start = Step(0, -1)
            stats(-1, start, 0)
            stats(-1, start, 1)
            first_half()

            def step(st):
                b, a, c, g = (st.item(lag) for lag in range(4))
                if st.ffn and not some(g):
                    dve.wait_ge(w_lo, NW)
                    dve.memset(act_[:, F:FPAD], 0.0).then_inc(filled, 1)
                for s in range(SLOTS):
                    if st.new:
                        hf, r = divmod(s, 8)
                        if r == 0 and some(2 * b + hf - 1):
                            dve.wait_ge(mrow_t, 2 * b + hf - 1)
                        dve.wait_ge(s_mm, 16 * b + s + 1)
                        dve.tensor_reduce(mx[:, hf, 2 * r:2 * r + 2], S[s % 2][:, :, :], AX.X, ALU.max,
                                          negate=True).then_inc(s_max, 1)
                    if st.att and s == 2:
                        mrow_parts(a, 1)
                    if st.ffn:
                        if s == 3:
                            compare(g, 3, gs[:, :], 4, cmp4)
                        if s == 4:
                            compare(g, 8, m8[:, :], 8, cmp8)
                        if s in (8, 11, 12, 13):
                            act_low(g, (8, 11, 12, 13).index(s))
                        if s in (1, 3, 6, 8):
                            gate_block(g, (1, 3, 6, 8).index(s))
                        if s in (2, 5, 7, 9):
                            up_block(g, (2, 5, 7, 9).index(s))
                        if s == 2:
                            router_scores(g)
                        if s == 3:
                            rank(g, 5, 4, cmp4, cst[:, C_L4:C_L4 + 16], rk4[:, :])
                            keep_groups(g)
                    if st.comb:
                        if s in (4, 6):
                            attention_out(c, s // 6)
                        if s == 10:
                            residual(c, x1[st.buf(2)])
                    if st.ffn and s == 4:
                        rank(g, 10, 8, cmp8, cst[:, C_L8:C_L8 + 64], rk8[:, :])
                        keep_experts(g)
                    if st.new and s == 10:
                        mrow_parts(b, 0)
                    if st.comb:
                        if s == 10:
                            residual_stats(c, x1[st.buf(2)])
                        if s == 12:
                            normal_h(c, x1[st.buf(2)])
                        if s == 14:
                            h_low(c)
                    if st.prep and s in (0, 13):
                        stats(-1, st, s // 13)
                    if (st.filling, s) in low_at:
                        weights_low(low_at.index((st.filling, s)))
                if st.ffn:
                    dve.wait_ge(y_mm, g + 1)
                    if some(16 * g):
                        dve.wait_ge(out_done, 16 * g)
                    dve.scalar_tensor_tensor(yo, GU[:, 1, 0:L], tg[:, 1:2], x1[st.buf(3)][:, :], ALU.mult,
                                             ALU.add).then_inc(y_done, 1)

            dve.wait_ge(gates_done, 1)
            steps(dve, step)

        @block.tensor
        def _(pe):
            def scores_n(st, s):
                b, n = st.item(0), st.buf(0)
                hf = s // 8
                if s % 8 < 4:
                    pe.wait_ge(qmask, 8 * b + 4 * hf + s % 4 + 1)
                if s % 8 == 0:
                    pe.wait_ge(k_done, 2 * b + hf + 1)
                if some(16 * b + s - 1):
                    pe.wait_ge(s_max, 16 * b + s - 1)
                for tc in range(2):
                    mm = pe.matmul(S[s % 2][:, tc, :], qm[n][0:ROWS, s, 128 * tc:128 * tc + 128],
                                   ks[n][0:ROWS, s // 4, :], start=True, stop=True)
                mm.then_inc(s_mm, 1)

            def mrow_turn(b, hf):
                pe.wait_ge(s_max, 16 * b + 8 * (hf + 1))
                pe.transpose(rows_turned[hf], mx[:, hf, :], ident).then_inc(mrow_t, 1)

            def scores_a(st, s):
                a, n = st.item(1), st.buf(1)
                p, kc = divmod(s, 2)
                if s % 8 == 0:
                    pe.wait_ge(mrow_in[s // 8], 32 * (a + 1))
                if some(16 * a + s - 1):
                    pe.wait_ge(exp_done, 16 * a + s - 1)
                pe.matmul(ST[s % 2][:, :], ks[n][:, p // 2, 128 * kc:128 * kc + 128],
                          qm[n][:, 2 * p:2 * p + 2, :], start=True, stop=True).then_inc(st_mm, 1)

            def values(a, n, q):
                pe.wait_ge(exp_done, 16 * a + 4 * q + 4)
                if q == 0:
                    pe.wait_ge(v_done, a + 1)
                if q % 2 == 0:
                    if some(2 * a + q // 2):
                        pe.wait_ge(av_sb, 2 * a + q // 2)
                for kc in range(2):
                    for i in range(4):
                        mm = pe.matmul(AV[32 * i:32 * i + 32, L * (q % 2):L * (q % 2) + L],
                                       vt[n][:, kc, 4 * q + i, :],
                                       probs[:, (4 * q + 2 * (i // 2) + kc) % 8, L * (i % 2):L * (i % 2) + L],
                                       start=(kc == 0), stop=(kc == 1))
                mm.then_inc(av_mm, 1)

            def gate_up(f, u):
                j, up = divmod(u, 2)
                if u == 0:
                    pe.wait_ge(hTl_done, f + 1)
                if j:
                    pe.wait_ge(act_done if up else tmp_done, 4 * f + j)
                elif up and some(f):
                    pe.wait_ge(y_done, f)
                c0, width = gate_up_columns(j, up)
                n = 0
                for kc in range(2):
                    for lhs, rhs in ((hTh, wguh), (hTh, wgul), (hTl, wguh)):
                        mm = pe.matmul(GU[:, up, 0:width], lhs[:, kc, :], rhs[:, kc, c0:c0 + width],
                                       start=(n == 0), stop=(n == 5))
                        n += 1
                mm.then_inc(gu_mm, 1)

            def act_turn(f, k):
                pe.wait_ge(act_done, 4 * f + (2, 3, 4, 4)[k])
                n = min(4, NC - 4 * k)
                for c in range(4 * k, 4 * k + n):
                    mm = pe.transpose(turned[k][:, 128 * (c % 4):128 * (c % 4) + 128],
                                      act_[:, 128 * c:128 * c + 128], ident)
                mm.then_inc(act_t, 1)

            def attention_turn(c, tc):
                pe.wait_ge(av_sb, 2 * c + 2)
                for q in range(GROUPS):
                    mm = pe.transpose(M1[:, 128 * q:128 * q + 128], avsb[:, q, 128 * tc:128 * tc + 128], ident)
                mm.then_inc(av_t, 1)

            def attention_back(c):
                pe.wait_ge(a_norm, 2 * c + 2)
                for tc in range(2):
                    mm = pe.transpose(G[:, 128 * tc:128 * tc + 128],
                                      aT[:, tc, :, :].rearrange("p h d -> p (h d)"), ident)
                mm.then_inc(a_back, 1)

            def h_turn(c):
                pe.wait_ge(h_done, c + 1)
                for kc in range(2):
                    mm = pe.transpose(G[:, 128 * kc:128 * kc + 128], h[:, 128 * kc:128 * kc + 128], ident)
                mm.then_inc(h_t, 1)

            def down(f, c0, c1):
                pe.wait_ge(aTl_done, 4 * f + (c1 + 3) // 4)
                if c0 == 0:
                    pe.wait_ge(act_done, 4 * f + 4)
                for c in range(c0, c1):
                    K = min(128, F - 128 * c)
                    for n, (lhs, rhs) in enumerate(((aTh, wdh), (aTh, wdl), (aTl, wdh))):
                        mm = pe.matmul(GU[:, 1, 0:L], lhs[0:K, c, :], rhs[0:K, c, :],
                                       start=(c == 0 and n == 0), stop=(c == NC - 1 and n == 2))
                if c1 == NC:
                    mm.then_inc(y_mm, 1)

            pe.wait_ge(const_in, 16)

            def step(st):
                b, a, c, g = (st.item(lag) for lag in range(4))
                if st.filling == 1:
                    pe.wait_ge(filled, 2)
                if st.ffn and not some(g):
                    pe.wait_ge(w_lo, NW)
                for s in range(SLOTS):
                    if st.new:
                        scores_n(st, s)
                    if st.att:
                        scores_a(st, s)
                        if s in (4, 9, 13):
                            values(a, st.buf(1), (4, 9, 13).index(s))
                    if st.comb and s == 1:
                        values(c, st.buf(2), 3)
                    if st.ffn and s in (0, 1, 2, 3, 5, 6, 7, 8):
                        gate_up(g, (0, 1, 2, 3, 5, 6, 7, 8).index(s))
                    if st.ffn and s >= 10:
                        down(g, *((0, 2), (2, 4), (4, 7), (7, 8), (8, 11), (11, NC))[s - 10])
                    if s == 1 and st.att:
                        if st.ffn and some(4 * g):
                            pe.wait_ge(aTl_done, 4 * g)
                        elif some(2 * c):
                            pe.wait_ge(a_norm, 2 * c)
                        elif some(2 * a):
                            pe.wait_ge(mrow_sb, 2 * a)
                        mrow_turn(a, 1)
                    if s == 3 and st.comb:
                        if st.att:
                            pe.wait_ge(mrow_sb, 2 * a + 2)
                        else:
                            pe.wait_ge(aTl_done, 4 * g)
                        attention_turn(c, 0)
                    if s == 5 and st.comb:
                        pe.wait_ge(a_norm, 2 * c + 1)
                        attention_turn(c, 1)
                    if s == 7 and st.ffn:
                        if st.comb:
                            pe.wait_ge(a_norm, 2 * c + 2)
                        else:
                            pe.wait_ge(aTl_done, 4 * g)
                        act_turn(g, 0)
                    if s == 10 and st.ffn:
                        pe.wait_ge(aTl_done, 4 * g + 1)
                        act_turn(g, 1)
                    if s == 12 and st.ffn:
                        pe.wait_ge(aTl_done, 4 * g + 2)
                        act_turn(g, 3)
                    if s == 9:
                        if st.ffn:
                            pe.wait_ge(tmp_done, 4 * g + 4)
                        elif some(2 * b - 1):
                            pe.wait_ge(mrow_sb, 2 * b - 1)
                        if st.comb:
                            attention_back(c)
                        if st.new:
                            mrow_turn(b, 0)
                    if s == 11 and st.ffn:
                        if st.comb:
                            pe.wait_ge(x1_done, c + 1)
                        if st.new:
                            pe.wait_ge(mrow_sb, 2 * b + 1)
                        act_turn(g, 2)
                    if s == 13 and st.comb:
                        if st.ffn:
                            pe.wait_ge(aTl_done, 4 * g + 3)
                        h_turn(c)

            steps(pe, step)


def constants():
    import numpy as np

    c = np.zeros((128, C_ALL), np.float32)
    c[:, C_ID:C_ID + 128] = np.eye(128)
    for i in range(4):
        c[:, C_MASK + i] = (np.arange(128) % 32) // CH == i
    c[:, C_L4:C_L4 + 16] = np.tril(np.ones((4, 4)), -1).reshape(1, 16)
    c[:, C_L8:C_L8 + 64] = np.tril(np.ones((8, 8)), -1).reshape(1, 64)
    return c


def kernel(x, ctx_2048, g_xattn, g_ffn, L0_ffn_gate_weight, L0_ffn_gate_w, L0_ffn_up_w, L0_ffn_down_w,
           L0_ffn_sh_gate_w, L0_ffn_sh_up_w, L0_ffn_sh_down_w):
    import numpy as np
    import concourse.bacc as bacc
    from concourse.bass_utils import run_bass_kernel_spmd

    a = np.asarray
    gate = np.concatenate([a(L0_ffn_sh_gate_w), a(L0_ffn_gate_w).reshape(-1, L)]).T
    up = np.concatenate([a(L0_ffn_sh_up_w), a(L0_ffn_up_w).reshape(-1, L)]).T
    cols = []
    for j, (first, width) in enumerate(zip(FIRST, BLOCKS)):
        cols.append(gate[:, first:first + width])
        if j == 0:
            cols.append(a(L0_ffn_gate_weight).T)
        cols.append(up[:, first:first + width])
    wd = np.zeros((FPAD, L), np.float32)
    wd[0:FS] = a(L0_ffn_sh_down_w).T
    wd[FS:F] = a(L0_ffn_down_w).transpose(0, 2, 1).reshape(-1, L)
    arrays = {
        "x": a(x),
        "y": a(ctx_2048),
        "yT": np.ascontiguousarray(a(ctx_2048).transpose(0, 2, 1)),
        "gx": a(g_xattn),
        "gf": a(g_ffn),
        "wgu": np.ascontiguousarray(np.concatenate(cols, axis=1)),
        "wd": wd,
        "consts": constants(),
    }
    nc = bacc.Bacc("TRN2", target_bir_lowering=False, num_devices=1)
    args = [nc.dram_tensor(n, v.shape, mybir.dt.from_np(v.dtype), kind="ExternalInput").ap()
            for n, v in arrays.items()]
    out = nc.dram_tensor("out", (B, W, L), F32, kind="ExternalOutput").ap()
    flamingo_kernel(nc, *args, out)
    r = run_bass_kernel_spmd(nc, [arrays], core_ids=[0])
    return r.results[0]["out"]
```

```python
from contextlib import ExitStack

import concourse.bass as bass
from concourse import mybir

F32 = mybir.dt.float32
F32R = mybir.dt.float32r
ALU = mybir.AluOpType
ACT = mybir.ActivationFunctionType
AX = mybir.AxisListType

B, W, L = 8, 128, 256
HEADS, CH = 16, 8
GROUPS = 4
EXPERTS, FE, FS = 8, 176, 352
F = FS + EXPERTS * FE
BLOCKS = (FS, 470, 470, 468)
FIRST = (0, FS, FS + 470, FS + 940)
assert sum(BLOCKS) == F
NC = (F + 127) // 128
FPAD = NC * 128
EPS = 1e-5
PARTS = 3
ROWS = 32 * PARTS
KROWS = ROWS + 2
SLOTS = 16
VCOL = 32

C_ID, C_MASK, C_L4, C_L8 = 0, 128, 132, 148
C_ALL = 212


def expert_segments(j):
    edges = [0] + [FS + e * FE for e in range(EXPERTS + 1)]
    out = []
    for n in range(EXPERTS + 1):
        a, b = max(edges[n], FIRST[j]), min(edges[n + 1], FIRST[j] + BLOCKS[j])
        if a < b:
            out.append((a - FIRST[j], b - FIRST[j], n - 1 if n else None))
    return out


def gate_up_columns(j, up):
    if (j, up) == (0, 0):
        return 0, BLOCKS[0] + EXPERTS
    return EXPERTS + 2 * FIRST[j] + up * BLOCKS[j], BLOCKS[j]


def some(count):
    return not isinstance(count, int) or count > 0


class Step:

    def __init__(self, r, par, prep=True, new=True, att=True, comb=True, ffn=True, filling=None):
        self.r, self.par = r, par
        self.prep, self.new, self.att, self.comb, self.ffn = prep, new, att, comb, ffn
        self.filling = filling

    def item(self, lag):
        return 2 * self.r + (self.par - lag)

    def buf(self, lag):
        return (self.par - lag) % 2

    def uses(self, lag):
        return self.r + (self.par - lag) // 2


def flamingo_kernel(nc, x, y, yT, gx, gf, wgu, wd, consts, out):
    with ExitStack() as ctx:
        def sb(name, shape, dt=F32):
            return ctx.enter_context(nc.sbuf_tensor(name, shape, dt))

        def ps(name, shape):
            return ctx.enter_context(nc.psum_tensor(name, shape, F32))

        def sem(name):
            return ctx.enter_context(nc.semaphore(name))

        cst = sb("cst", [128, C_ALL])
        ident = cst[:, C_ID:C_ID + 128]
        wguh = sb("wguh", [128, 2, 2 * F + EXPERTS], F32R)
        wgul = sb("wgul", [128, 2, 2 * F + EXPERTS], F32R)
        wdh = sb("wdh", [128, NC, L], F32R)
        wdl = sb("wdl", [128, NC, L], F32R)
        gates = sb("gates", [128, 2])
        tg = sb("tg", [128, 2])
        xs = [sb(f"xs{n}", [ROWS, GROUPS, L]) for n in range(2)]
        kr = [sb(f"kr{n}", [ROWS, GROUPS, L]) for n in range(2)]
        parts = sb("parts", [ROWS, 2, L], F32R)
        qr = parts[64:96, :, :]
        mh, ml = (parts[0:SLOTS, n, :].rearrange("p (c t) -> p c t", t=128) for n in range(2))
        qm = [sb(f"qm{n}", [KROWS, HEADS, L], F32R) for n in range(2)]
        ks = [sb(f"ks{n}", [KROWS, GROUPS, L], F32R) for n in range(2)]
        vraw = sb("vraw", [128, 2, W])
        vt = [sb(f"vt{n}", [128, 2, HEADS, VCOL]) for n in range(2)]
        pst = sb("pst", [ROWS, 2, 2, 6])
        pmv = sb("pmv", [ROWS, 2, 2, 2])
        pve = sb("pve", [ROWS, 2, 2])
        prs = sb("prs", [ROWS, 2, 2])
        mhalf = sb("mhalf", [128, 2])
        zero = sb("zero", [128, 1])
        unused = sb("unused", [1, 1])
        warm = sb("warm", [128, 1])
        mx = sb("mx", [128, 2, SLOTS])
        probs = sb("probs", [128, 8, 512])
        avsb = sb("avsb", [128, GROUPS, L])
        rec = sb("rec", [128, 2, HEADS])
        aT = sb("aT", [128, 2, HEADS, CH])
        xr = sb("xr", [128, L])
        x1 = [sb(f"x1{n}", [128, L]) for n in range(2)]
        h = sb("h", [128, L])
        fst = sb("fst", [128, 6])
        fmv = sb("fmv", [128, 2])
        fve = sb("fve", [128, 1])
        frs = sb("frs", [128, 1])
        hTh = sb("hTh", [128, 2, W], F32R)
        hTl = sb("hTl", [128, 2, W], F32R)
        lg = sb("lg", [128, EXPERTS])
        nm = sb("nm", [128, 1])
        e8 = sb("e8", [128, EXPERTS])
        es = sb("es", [128, 1])
        er = sb("er", [128, 1])
        sc = sb("sc", [128, EXPERTS])
        gs = sb("gs", [128, 4])
        cmp4 = sb("cmp4", [128, 4, 2 * 4])
        rk4 = sb("rk4", [128, 4])
        m8 = sb("m8", [128, EXPERTS])
        cmp8 = sb("cmp8", [128, 8, 2 * 8])
        rk8 = sb("rk8", [128, EXPERTS])
        w8 = sb("w8", [128, EXPERTS])
        thy = sb("thy", [128, 2 * max(BLOCKS) + L])
        th = thy[:, 0:2 * max(BLOCKS)].rearrange("p (n c) -> p n c", n=2)
        yo = thy[:, 2 * max(BLOCKS):]
        tmp = sb("tmp", [128, max(BLOCKS)])
        act_ = sb("act_", [128, 4 * max(BLOCKS)])
        aTh = sb("aTh", [128, NC, W], F32R)
        aTl = sb("aTl", [128, NC, W], F32R)

        wst = [thy[:, 0:2 * max(BLOCKS)], act_[:, 0:2 * max(BLOCKS)], act_[:, 2 * max(BLOCKS):]]

        S = [ps(f"S{n}", [128, 2, L]) for n in range(2)]
        ST = [ps(f"ST{n}", [128, 512]) for n in range(2)]
        GU = ps("GU", [128, 2, 512])
        AV = ps("AV", [128, 512])
        M1 = ps("M1", [128, 512])
        G = GU[:, 0, :]

        const_in, gates_in = sem("const_in"), sem("gates_in")
        w_in = [sem(f"w_in{n}") for n in range(3)]
        w_hi = sem("w_hi")
        w_lo, w_lo_pool = sem("w_lo"), sem("w_lo_pool")
        x_in = [sem(f"x_in{n}") for n in range(2)]
        y_in = [sem(f"y_in{n}") for n in range(2)]
        mrow_in = [sem(f"mrow_in{n}") for n in range(2)]
        v_in, xr_in, out_done = sem("v_in"), sem("xr_in"), sem("out_done")
        gates_done, filled = sem("gates_done"), sem("filled")
        pool_filled, zero_filled = sem("pool_filled"), sem("zero_filled")
        p_bn, p_mv, p_ve, p_rstd, p_mid, p_q = (
            sem(f"p_{s}") for s in ("bn", "mv", "ve", "rstd", "mid", "q"))
        p_qr, p_lo, qmask = sem("p_qr"), sem("p_lo"), sem("qmask")
        k_hi, k_done, v_done = sem("k_hi"), sem("k_done"), sem("v_done")
        s_mm, s_max, mrow_t, mrow_hi, mrow_sb = (
            sem(n) for n in ("s_mm", "s_max", "mrow_t", "mrow_hi", "mrow_sb"))
        st_mm, exp_done, av_mm, av_sb = sem("st_mm"), sem("exp_done"), sem("av_mm"), sem("av_sb")
        av_t, a_rec, a_norm, a_back = sem("av_t"), sem("a_rec"), sem("a_norm"), sem("a_back")
        x1_done, f_bn, f_mv, f_ve, f_rstd = (
            sem(n) for n in ("x1_done", "f_bn", "f_mv", "f_ve", "f_rstd"))
        h_done, h_t, hTh_done, hTl_done = sem("h_done"), sem("h_t"), sem("hTh_done"), sem("hTl_done")
        gu_mm, lg_done, nm_done, e8_done, th_done = (
            sem(n) for n in ("gu_mm", "lg_done", "nm_done", "e8_done", "th_done"))
        routed = sem("routed")
        w8_done = sem("w8_done")
        tmp_done, act_done, act_t, aTh_done, aTl_done = (
            sem(n) for n in ("tmp_done", "act_done", "act_t", "aTh_done", "aTl_done"))
        y_mm, y_done = sem("y_mm"), sem("y_done")

        block = ctx.enter_context(nc.Block())

        def steps(eng, step):
            step(Step(0, 0, att=False, comb=False, ffn=False, filling=0))
            step(Step(0, 1, comb=False, ffn=False, filling=1))
            step(Step(1, 0, ffn=False, filling=2))
            step(Step(1, 1))
            with eng.Fori(2, B // 2) as r:
                for par in range(2):
                    step(Step(r, par))
            step(Step(B // 2, 0, prep=False, new=False))
            step(Step(B // 2, 1, prep=False, new=False, att=False))
            step(Step(B // 2 + 1, 0, prep=False, new=False, att=False, comb=False))

        def stacked(src, b):
            return src[b].rearrange("(g p) l -> p g l", p=32)

        wgu_v = wgu.rearrange("(c p) n -> p c n", p=128)
        pieces = []
        for u in range(8):
            a, width = gate_up_columns(*divmod(u, 2))
            pieces.append((wgu_v[:, :, a:a + width], wguh[:, :, a:a + width], wgul[:, :, a:a + width]))
        wd_v = wd.rearrange("(c p) n -> p c n", p=128)
        for a in range(0, NC, 3):
            z = min(a + 3, NC)
            pieces.append((wd_v[:, a:z, :], wdh[:, a:z, :], wdl[:, a:z, :]))
        NW = len(pieces)

        def staged(n):
            c, width = pieces[n][1].shape[1:]
            return wst[n % 3][:, 0:c * width].rearrange("p (c n) -> p c n", n=width)

        loaded_at = {(0, 5): 3, (0, 9): 4, (0, 12): 5, (1, 1): 6, (1, 3): 7, (1, 5): 8, (1, 9): 9, (1, 13): 10,
                     (2, 0): 11, (2, 1): 12}
        rounded_at = {(0, 2): 0, (0, 7): 1, (0, 9): 2, (0, 11): 3, (1, 0): 4, (1, 2): 5, (1, 7): 6, (1, 8): 7,
                      (1, 11): 8, (1, 13): 9, (2, 2): 10, (2, 7): 11, (2, 8): 12}
        low_at = {(0, 4): 0, (0, 8): 1, (0, 11): 2, (1, 2): 4, (1, 4): 5, (1, 8): 6, (1, 12): 7,
                  (1, 15): 9, (2, 4): 10, (2, 9): 11}
        by_gpsimd = (3, 8, 12)

        def by_vector(n):
            return n + 1 - sum(m <= n for m in by_gpsimd)

        def scores_bank(st, s):
            if st.filling is None:
                return S[s % 2]
            return (S[0], S[1], GU[:, 1, :].rearrange("p (c n) -> p c n", n=L))[(SLOTS * st.filling + s) % 3]

        def gate_bank(st, j):
            return G if st.new or j % 2 == 0 else S[0][:, :, :].rearrange("p c n -> p (c n)")

        def up_bank(st, j):
            return GU[:, 1, :] if st.new or j % 2 == 0 else S[1][:, :, :].rearrange("p c n -> p (c n)")

        turned = (M1, M1, G, M1)
        rows_turned = (G[0:SLOTS, L:L + 128], M1[0:SLOTS, 0:128])

        @block.sync
        def _(sp):
            def load_x(n, src):
                for j in range(PARTS):
                    sp.dma_start(xs[n][32 * j:32 * j + 32, :, :], stacked(x, src)).then_inc(x_in[n], 16)

            def load_y(n, src):
                for j in range(PARTS):
                    sp.dma_start(kr[n][32 * j:32 * j + 32, :, :], stacked(y, src)).then_inc(y_in[n], 16)

            def load_v(src):
                sp.dma_start(vraw[:, :, :], yT[src].rearrange("(c p) w -> p c w", p=128)).then_inc(v_in, 16)

            load_x(0, 0)
            sp.dma_start(cst[:, :], consts).then_inc(const_in, 16)
            load_y(0, 0)
            sp.dma_start(gates[:, 0:1], gx.partition_broadcast(128)).then_inc(gates_in, 16)
            sp.dma_start(gates[:, 1:2], gf.partition_broadcast(128)).then_inc(gates_in, 16)
            load_v(0)
            load_x(1, 1)
            load_y(1, 1)
            for n in range(3):
                sp.dma_start(staged(n), pieces[n][0]).then_inc(w_in[n], 16)

            def mrow(b, n, hf):
                sp.wait_ge(mrow_sb, 2 * b + hf + 1)
                for row, part in enumerate((mh, ml)):
                    dst = qm[n][ROWS + row:ROWS + row + 1, 8 * hf:8 * hf + 8, :]
                    sp.dma_start(dst.rearrange("o h (c t) -> o (h c) t", t=128).bitcast(F32),
                                 part[:, hf, :].bitcast(F32)).then_inc(mrow_in[hf], 16)

            def step(st):
                b, a, c, g = (st.item(lag) for lag in range(4))
                if st.comb:
                    if some(c):
                        sp.wait_ge(x1_done, c)
                    sp.dma_start(xr[:, :], x[c]).then_inc(xr_in, 16)
                if st.att:
                    mrow(a, st.buf(1), 1)
                if st.new:
                    sp.wait_ge(v_done, b + 1)
                    load_v((b + 1) % B)
                    sp.wait_ge(qmask, 8 * (b + 1))
                    load_x(st.buf(0), (b + 2) % B)
                    sp.wait_ge(k_done, 2 * (b + 1))
                    load_y(st.buf(0), (b + 2) % B)
                    mrow(b, st.buf(0), 0)
                if st.ffn:
                    sp.wait_ge(y_done, g + 1)
                    sp.dma_start(out[g], yo).then_inc(out_done, 16)

            steps(sp, step)
            sp.wait_ge(out_done, 16 * B)

        @block.gpsimd
        def _(pool):
            pool.memset(zero[:, :], 0.0).then_inc(zero_filled, 1)
            pool.memset(mhalf[:, :], -0.5).then_inc(pool_filled, 1)
            for n in range(2):
                pool.memset(vt[n][:, :, :, CH + 1:VCOL], 0.0).then_inc(pool_filled, 1)
                pool.memset(vt[n][:, :, :, CH:CH + 1], 1.0).then_inc(pool_filled, 1)

            def copy(dst, src):
                p = src.start_partition()
                z = zero[p:p + src.shape[0], :]
                while len(z.shape) < len(src.shape):
                    z = z.unsqueeze(1)
                return pool.tensor_tensor(dst, src, z.to_broadcast(list(src.shape)), ALU.add)


            def rstd(lag, st, hf, last, count):
                n = 2 * st.item(lag) + hf
                pool.wait_ge(p_ve, n + 1)
                pool.wait_ge(last, count)
                pool.tensor_tensor(prs[:, hf, :], pve[:, hf, :], mhalf[0:ROWS, :], ALU.pow).then_inc(p_rstd, 1)

            def normal(lag, st, hf):
                n = 2 * st.item(lag) + hf
                q = xs[st.buf(lag)][:, 2 * hf:2 * hf + 2, :]
                pool.wait_ge(p_rstd, n + 1)
                pool.tensor_tensor(q, q, pmv[:, hf, :, 0:1].to_broadcast([ROWS, 2, L]),
                                   ALU.subtract).then_inc(p_mid, 1)
                pool.wait_ge(p_mid, n - 1)
                pool.tensor_tensor(q, q, prs[:, hf, :].unsqueeze(2).to_broadcast([ROWS, 2, L]),
                                   ALU.mult).then_inc(p_q, 1)

            def q_low(lag, st, hf):
                n = 2 * st.item(lag) + hf
                q = xs[st.buf(lag)][64:96, 2 * hf:2 * hf + 2, :]
                pool.wait_ge(p_q, n + 1)
                copy(qr, q).then_inc(p_qr, 1)
                pool.wait_ge(p_qr, n + 1)
                pool.tensor_tensor(q, q, qr.bitcast(F32), ALU.subtract).then_inc(p_lo, 1)

            def k_parts(lag, st, hf, last, count):
                b, n = st.item(lag), st.buf(lag)
                pool.wait_ge(last, count)
                src = kr[n][:, 2 * hf:2 * hf + 2, :]
                dst = ks[n][:, 2 * hf:2 * hf + 2, :]
                if hf == 0:
                    pool.wait_ge(y_in[n], 48 * (st.uses(lag) + 1))
                if some(16 * (b - 2) + 8 * (hf + 1)):
                    pool.wait_ge(st_mm, 16 * (b - 2) + 8 * (hf + 1))
                copy(dst[0:ROWS], src).then_inc(k_hi, 1)
                pool.wait_ge(k_hi, 2 * b + hf + 1)
                pool.tensor_tensor(dst[32:64], src[32:64], dst[32:64].bitcast(F32),
                                   ALU.subtract).then_inc(k_done, 1)

            def values(st):
                b = st.item(0)
                pool.wait_ge(v_in, 16 * (b + 1))
                pool.wait_ge(k_done, 2 * b + 2)
                if some(4 * (b - 1)):
                    pool.wait_ge(av_mm, 4 * (b - 1))
                copy(vt[st.buf(0)][:, :, :, 0:CH],
                     vraw[:, :, :].rearrange("p c (h d) -> p c h d", d=CH)).then_inc(v_done, 1)

            def weights_low(n):
                _, hi, lo = pieces[n]
                pool.wait_ge(w_hi, n + 1)
                pool.tensor_tensor(lo, staged(n), hi.bitcast(F32), ALU.subtract).then_inc(w_lo_pool, 1)

            pool.wait_ge(zero_filled, 1)
            pool.wait_ge(pool_filled, 5)
            start = Step(0, -1)
            rstd(-1, start, 0, pool_filled, 5)
            rstd(-1, start, 1, p_rstd, 1)
            pool.wait_ge(p_lo, 1)
            q_low(-1, start, 1)

            def step(st):
                b, c = st.item(0), st.item(2)
                if st.new:
                    k_parts(0, st, 1, p_lo, 2 * b + 2)
                    values(st)
                if st.prep:
                    rstd(-1, st, 0, v_done, b + 1)
                    normal(-1, st, 0)
                    q_low(-1, st, 0)
                    if st.filling != 0:
                        k_parts(-1, st, 0, p_lo, 2 * b + 3)
                if st.comb:
                    pool.wait_ge(f_ve, c + 1)
                    if st.prep:
                        pool.wait_ge(k_done, 2 * b + 3)
                    else:
                        pool.wait_ge(p_lo, 2 * (B + 1))
                    pool.tensor_tensor(frs[:, :], fve[:, :], mhalf[:, 0:1], ALU.pow).then_inc(f_rstd, 1)
                    pool.wait_ge(f_rstd, c + 1)
                if st.prep:
                    last, count = (f_rstd, c + 1) if st.comb else (p_lo, 2 * b + 3)
                    if st.filling is not None:
                        if st.filling == 1:
                            pool.wait_ge(k_done, 2 * b + 3)
                        pool.wait_ge(last, count)
                        weights_low(by_gpsimd[st.filling])
                        last, count = w_lo_pool, st.filling + 1
                    rstd(-1, st, 1, last, count)
                    normal(-1, st, 1)
                    q_low(-1, st, 1)

            steps(pool, step)

        @block.scalar
        def _(act):
            def masks(lag, st, hf, i):
                b, n = st.item(lag), st.buf(lag)
                if i == 0:
                    act.wait_ge(p_lo, 2 * b + hf + 1)
                    if some(16 * (b - 2) + 8 * (hf + 1)):
                        act.wait_ge(st_mm, 16 * (b - 2) + 8 * (hf + 1))
                dst = qm[n][0:ROWS, 8 * hf:8 * hf + 8, :].rearrange("p (g i) t -> p i g t", i=4)
                act.activation(dst[:, i, :, :], xs[n][:, 2 * hf:2 * hf + 2, :], ACT.Copy,
                               scale=cst[0:ROWS, C_MASK + i:C_MASK + i + 1]).then_inc(qmask, 1)

            def round_piece(n):
                act.wait_ge(w_in[n % 3], 16 * (n // 3 + 1))
                act.activation(pieces[n][1], staged(n), ACT.Copy).then_inc(w_hi, 1)

            def load_piece(n):
                if n - 3 in by_gpsimd:
                    act.wait_ge(w_lo_pool, by_gpsimd.index(n - 3) + 1)
                else:
                    act.wait_ge(w_lo, by_vector(n - 3))
                act.dma_start(staged(n), pieces[n][0]).then_inc(w_in[n % 3], 16)

            act.wait_ge(zero_filled, 1)
            act.activation(warm[:, :], zero[:, :], ACT.Exp)
            act.wait_ge(const_in, 16)
            for i in range(4):
                masks(-1, Step(0, -1), 0, i)
            act.wait_ge(gates_in, 32)
            act.activation(tg[:, :], gates[:, :], ACT.Tanh).then_inc(gates_done, 1)

            def tanh_block(st, g, j):
                act.wait_ge(gu_mm, 8 * g + 2 * j + 1)
                if j == 0:
                    act.activation(lg[:, :], GU[:, 0, FS:FS + EXPERTS], ACT.Copy).then_inc(lg_done, 1)
                if j >= 2:
                    act.wait_ge(tmp_done, 4 * g + j - 1)
                act.activation(th[:, j % 2, 0:BLOCKS[j]], gate_bank(st, j)[:, 0:BLOCKS[j]], ACT.Tanh,
                               scale=0.5).then_inc(th_done, 1)
                if j == 0:
                    act.wait_ge(nm_done, g + 1)
                    act.activation(e8[:, :], lg[:, :], ACT.Exp, bias=nm[:, 0:1],
                                   accum_out=es[:, :]).then_inc(e8_done, 1)

            def act_high(g, k):
                n = min(4, NC - 4 * k)
                act.wait_ge(act_t, 4 * g + k + 1)
                act.activation(aTh[:, 4 * k:4 * k + n, :], turned[k][:, 0:128 * n], ACT.Copy).then_inc(aTh_done, 1)

            def attention_copy(a, k):
                act.wait_ge(av_mm, 4 * a + 2 * k + 2)
                if k == 0 and some(2 * a):
                    act.wait_ge(av_t, 2 * a)
                act.activation(avsb[:, 2 * k:2 * k + 2, :], AV[:, :], ACT.Copy).then_inc(av_sb, 1)

            def step(st):
                b, a, c, g = (st.item(lag) for lag in range(4))
                if st.ffn and not some(g):
                    act.wait_ge(w_lo, by_vector(NW - 1))
                    act.wait_ge(w_lo_pool, len(by_gpsimd))
                for s in range(SLOTS):
                    if st.comb:
                        if s == 2:
                            attention_copy(c, 1)
                        if s == 14:
                            act.wait_ge(h_t, c + 1)
                            act.activation(hTh[:, :, :], G[:, 0:L], ACT.Copy).then_inc(hTh_done, 1)
                    if st.att and s == 10:
                        attention_copy(a, 0)
                    if st.ffn and s in (8, 11, 12, 13):
                        act_high(g, (8, 11, 12, 13).index(s))
                    if st.att:
                        act.wait_ge(st_mm, 16 * a + s + 1)
                        if s % 4 == 0 and some(4 * a + s // 4 - 1):
                            act.wait_ge(av_mm, 4 * a + s // 4 - 1)
                        act.activation(probs[:, s % 8, :], ST[s % 2][:, :], ACT.Exp).then_inc(exp_done, 1)
                    if st.ffn and s in (0, 2, 5, 7):
                        tanh_block(st, g, (0, 2, 5, 7).index(s))
                    if st.new and s in (3, 4, 5, 6):
                        masks(0, st, 1, s - 3)
                    masked_at = (12, 13, 14, 15) if st.filling == 0 else (9, 10, 14, 15)
                    if st.prep and s in masked_at:
                        masks(-1, st, 0, masked_at.index(s))
                    if (st.filling, s) in loaded_at:
                        load_piece(loaded_at[st.filling, s])
                    if (st.filling, s) in rounded_at:
                        round_piece(rounded_at[st.filling, s])

            steps(act, step)

        @block.vector
        def _(dve):
            def stats(lag, st, hf):
                b, n = st.item(lag), st.buf(lag)
                m = 2 * b + hf
                if hf == 0:
                    dve.wait_ge(x_in[n], 48 * (st.uses(lag) + 1))
                for g in range(2):
                    dve.bn_stats(pst[:, hf, g, :], xs[n][:, 2 * hf + g, :]).then_inc(p_bn, 1)
                dve.wait_ge(p_bn, 2 * m + 2)
                dve.memset(unused[:, :], 0.0)
                for g in range(2):
                    dve.bn_aggr(pmv[:, hf, g, :], pst[:, hf, g, :]).then_inc(p_mv, 1)
                dve.wait_ge(p_mv, 2 * m + 2)
                dve.tensor_scalar(pve[:, hf, :], pmv[:, hf, :, 1], EPS, float(CH), ALU.add,
                                  ALU.mult).then_inc(p_ve, 1)

            def first_normal(hf):
                dve.wait_ge(p_rstd, hf + 1)
                for g in range(2):
                    q = xs[0][:, 2 * hf + g, :]
                    ins = dve.tensor_scalar(q, q, pmv[:, hf, g, 0:1], prs[:, hf, g:g + 1], ALU.subtract, ALU.mult)
                ins.then_inc(p_q, 1)

            def first_keys(b):
                k, dst = kr[b][:, 0:2, :], ks[b][:, 0:2, :]
                dve.wait_ge(y_in[b], 48)
                if b:
                    dve.wait_ge(k_done, 2 * b)
                dve.tensor_copy(dst[0:ROWS], k).then_inc(k_hi, 1)
                dve.wait_ge(k_hi, 2 * b + 1)
                dve.tensor_tensor(dst[32:64], k[32:64], dst[32:64].bitcast(F32), ALU.subtract).then_inc(k_done, 1)

            def first_q_low():
                dve.wait_ge(p_q, 1)
                q = xs[0][64:96, 0:2, :]
                dve.tensor_copy(qr, q).then_inc(p_qr, 1)
                dve.wait_ge(p_qr, 1)
                dve.tensor_tensor(q, q, qr.bitcast(F32), ALU.subtract).then_inc(p_lo, 1)

            def mrow_parts(b, hf):
                n = 2 * b + hf
                dve.wait_ge(mrow_t, n + 1)
                if some(32 * b):
                    dve.wait_ge(mrow_in[hf], 32 * b)
                dve.tensor_copy(mh[:, hf, :], rows_turned[hf]).then_inc(mrow_hi, 1)
                dve.wait_ge(mrow_hi, n + 1)
                dve.tensor_tensor(ml[:, hf, :], rows_turned[hf], mh[:, hf, :].bitcast(F32),
                                  ALU.subtract).then_inc(mrow_sb, 1)

            def weights_low(n):
                _, hi, lo = pieces[n]
                dve.wait_ge(w_hi, n + 1)
                dve.tensor_tensor(lo, staged(n), hi.bitcast(F32), ALU.subtract).then_inc(w_lo, 1)

            def attention_out(c, tc):
                dve.wait_ge(av_t, 2 * c + tc + 1)
                v = M1[:, :].rearrange("p (h d) -> p h d", d=VCOL)
                dve.reciprocal(rec[:, tc, :], v[:, :, CH]).then_inc(a_rec, 1)
                dve.wait_ge(a_rec, 2 * c + tc + 1)
                dve.tensor_tensor(aT[:, tc, :, :], v[:, :, 0:CH],
                                  rec[:, tc, :].unsqueeze(2).to_broadcast([128, HEADS, CH]),
                                  ALU.mult).then_inc(a_norm, 1)

            def residual(c, x1c):
                dve.wait_ge(a_back, c + 1)
                dve.wait_ge(xr_in, 16 * (c + 1))
                dve.scalar_tensor_tensor(x1c[:, :], G[:, 0:L], tg[:, 0:1], xr[:, :], ALU.mult,
                                         ALU.add).then_inc(x1_done, 1)

            def residual_stats(c, x1c):
                dve.wait_ge(x1_done, c + 1)
                dve.bn_stats(fst[:, :], x1c[:, :]).then_inc(f_bn, 1)

            def residual_variance(c):
                dve.wait_ge(f_bn, c + 1)
                dve.memset(unused[:, :], 0.0)
                dve.bn_aggr(fmv[:, :], fst[:, :]).then_inc(f_mv, 1)
                dve.wait_ge(f_mv, c + 1)
                dve.tensor_scalar(fve[:, :], fmv[:, 1:2], EPS, None, ALU.add).then_inc(f_ve, 1)

            def normal_h(c, x1c):
                dve.wait_ge(f_rstd, c + 1)
                dve.tensor_scalar(h[:, :], x1c[:, :], fmv[:, 0:1], frs[:, 0:1], ALU.subtract,
                                  ALU.mult).then_inc(h_done, 1)

            def h_low(c):
                dve.wait_ge(hTh_done, c + 1)
                dve.tensor_tensor(hTl[:, :, :], G[:, 0:L].rearrange("p (c t) -> p c t", t=W),
                                  hTh[:, :, :].bitcast(F32), ALU.subtract).then_inc(hTl_done, 1)

            ROUTED = 12

            def router_scores(f):
                dve.wait_ge(e8_done, f + 1)
                dve.reciprocal(er[:, :], es[:, :]).then_inc(routed, 1)
                dve.wait_ge(routed, ROUTED * f + 1)
                dve.tensor_scalar(sc[:, :], e8[:, :], er[:, 0:1], 0.5, ALU.mult, ALU.mult).then_inc(routed, 1)
                dve.wait_ge(routed, ROUTED * f + 2)
                dve.tensor_reduce(gs[:, :], sc[:, :].rearrange("p (g e) -> p g e", e=2), AX.X,
                                  ALU.max).then_inc(routed, 1)

            def compare(f, done, v, size, cmp):
                other = v.unsqueeze(1).to_broadcast([128, size, size])
                own = v.unsqueeze(2).to_broadcast([128, size, size])
                dve.wait_ge(routed, ROUTED * f + done)
                dve.tensor_tensor(cmp[:, :, 0:size], other, own, ALU.is_gt).then_inc(routed, 1)
                dve.tensor_tensor(cmp[:, :, size:2 * size], other, own, ALU.is_equal).then_inc(routed, 1)

            def rank(f, done, size, cmp, lower, rk):
                dve.wait_ge(routed, ROUTED * f + done)
                dve.tensor_tensor(cmp[:, :, size:2 * size], cmp[:, :, size:2 * size],
                                  lower.rearrange("p (i j) -> p i j", j=size), ALU.mult).then_inc(routed, 1)
                dve.wait_ge(routed, ROUTED * f + done + 1)
                dve.tensor_reduce(rk, cmp[:, :, :], AX.X, ALU.add).then_inc(routed, 1)

            def keep_groups(f):
                dve.wait_ge(routed, ROUTED * f + 7)
                dve.scalar_tensor_tensor(m8[:, :].rearrange("p (g e) -> p g e", e=2),
                                         rk4[:, :].unsqueeze(2).to_broadcast([128, 4, 2]), 2.0,
                                         sc[:, :].rearrange("p (g e) -> p g e", e=2),
                                         ALU.is_lt, ALU.mult).then_inc(routed, 1)

            def keep_experts(f):
                dve.wait_ge(routed, ROUTED * f + 12)
                dve.scalar_tensor_tensor(w8[:, :], rk8[:, :], 2.0, m8[:, :], ALU.is_lt,
                                         ALU.mult).then_inc(w8_done, 1)

            def gate_block(st, f, j):
                if j == 0:
                    dve.wait_ge(lg_done, f + 1)
                    dve.tensor_reduce(nm[:, :], lg[:, :], AX.X, ALU.max, negate=True).then_inc(nm_done, 1)
                dve.wait_ge(th_done, 4 * f + j + 1)
                if j:
                    dve.wait_ge(act_done, 4 * f + j)
                dve.scalar_tensor_tensor(tmp[:, 0:BLOCKS[j]], th[:, j % 2, 0:BLOCKS[j]], 1.0,
                                         gate_bank(st, j)[:, 0:BLOCKS[j]], ALU.add, ALU.mult).then_inc(tmp_done, 1)

            def up_block(st, f, j):
                dve.wait_ge(gu_mm, 8 * f + 2 * j + 2)
                dve.wait_ge(tmp_done, 4 * f + j + 1)
                if j == 1:
                    dve.wait_ge(w8_done, f + 1)
                segments = expert_segments(j)
                for n, (c0, c1, e) in enumerate(segments):
                    ins = dve.scalar_tensor_tensor(
                        act_[:, FIRST[j] + c0:FIRST[j] + c1], tmp[:, c0:c1],
                        0.5 if e is None else w8[:, e:e + 1], up_bank(st, j)[:, c0:c1], ALU.mult, ALU.mult)
                    if n == len(segments) - 1:
                        ins.then_inc(act_done, 1)

            def act_low(f, k):
                n = min(4, NC - 4 * k)
                dve.wait_ge(aTh_done, 4 * f + k + 1)
                dve.tensor_tensor(aTl[:, 4 * k:4 * k + n, :], turned[k][:, 0:128 * n].rearrange("p (c t) -> p c t", t=128),
                                  aTh[:, 4 * k:4 * k + n, :].bitcast(F32), ALU.subtract).then_inc(aTl_done, 1)

            for n in range(2):
                dve.memset(ks[n][ROWS:KROWS, :, :].bitcast(F32), 1.0).then_inc(filled, 1)
            start = Step(0, -1)
            stats(-1, start, 0)
            first_normal(0)
            first_q_low()
            first_keys(0)
            stats(-1, start, 1)

            def step(st):
                b, a, c, g = (st.item(lag) for lag in range(4))
                if st.ffn and not some(g):
                    dve.wait_ge(w_lo_pool, len(by_gpsimd))
                    dve.memset(act_[:, F:FPAD], 0.0).then_inc(filled, 1)
                for s in range(SLOTS):
                    if st.ffn and s == 5:
                        up_block(st, g, 1)
                    if st.ffn and s == 11:
                        act_low(g, 1)
                    if st.new:
                        hf, r = divmod(s, 8)
                        if r == 0 and some(2 * b + hf - 1):
                            dve.wait_ge(mrow_t, 2 * b + hf - 1)
                        dve.wait_ge(s_mm, 16 * b + s + 1)
                        dve.tensor_reduce(mx[:, hf, 2 * r:2 * r + 2], scores_bank(st, s)[:, :, :], AX.X, ALU.max,
                                          negate=True).then_inc(s_max, 1)
                    if st.filling == 0 and s == 0:
                        first_normal(1)
                    if st.att and s == 2:
                        mrow_parts(a, 1)
                    if st.ffn:
                        if s == 3:
                            compare(g, 3, gs[:, :], 4, cmp4)
                        if s == 4:
                            compare(g, 8, m8[:, :], 8, cmp8)
                        if s in (8, 12, 13):
                            act_low(g, (8, 11, 12, 13).index(s))
                        if s in (1, 3, 6, 8):
                            gate_block(st, g, (1, 3, 6, 8).index(s))
                        if s in (2, 7, 9):
                            up_block(st, g, (2, 5, 7, 9).index(s))
                        if s == 2:
                            router_scores(g)
                        if s == 3:
                            rank(g, 5, 4, cmp4, cst[:, C_L4:C_L4 + 16], rk4[:, :])
                            keep_groups(g)
                    if st.comb:
                        if s in (4, 6):
                            attention_out(c, s // 6)
                        if s == 10:
                            residual(c, x1[st.buf(2)])
                    if st.ffn and s == 4:
                        rank(g, 10, 8, cmp8, cst[:, C_L8:C_L8 + 64], rk8[:, :])
                        keep_experts(g)
                    if st.new and s == 10:
                        mrow_parts(b, 0)
                    if st.comb:
                        if s == 10:
                            residual_stats(c, x1[st.buf(2)])
                        if s == 11:
                            residual_variance(c)
                        if s == 12:
                            normal_h(c, x1[st.buf(2)])
                        if s == 14:
                            h_low(c)
                    if st.prep and s in (0, 13):
                        stats(-1, st, s // 13)
                    if st.filling == 0 and s == 9:
                        first_keys(1)
                    if (st.filling, s) in low_at:
                        weights_low(low_at[st.filling, s])
                if st.ffn:
                    dve.wait_ge(y_mm, g + 1)
                    if some(16 * g):
                        dve.wait_ge(out_done, 16 * g)
                    dve.scalar_tensor_tensor(yo, GU[:, 1, 0:L], tg[:, 1:2], x1[st.buf(3)][:, :], ALU.mult,
                                             ALU.add).then_inc(y_done, 1)

            dve.wait_ge(gates_done, 1)
            steps(dve, step)

        @block.tensor
        def _(pe):
            def scores_n(st, s):
                b, n = st.item(0), st.buf(0)
                hf = s // 8
                if s % 8 < 4:
                    pe.wait_ge(qmask, 8 * b + 4 * hf + s % 4 + 1)
                if s % 8 == 0:
                    pe.wait_ge(k_done, 2 * b + hf + 1)
                read = 16 * b + s - (1 if st.filling is None else 2)
                if some(read):
                    pe.wait_ge(s_max, read)
                for tc in range(2):
                    mm = pe.matmul(scores_bank(st, s)[:, tc, :], qm[n][0:ROWS, s, 128 * tc:128 * tc + 128],
                                   ks[n][0:ROWS, s // 4, :], start=True, stop=True)
                mm.then_inc(s_mm, 1)

            def mrow_turn(b, hf):
                pe.wait_ge(s_max, 16 * b + 8 * (hf + 1))
                pe.transpose(rows_turned[hf], mx[:, hf, :], ident).then_inc(mrow_t, 1)

            def scores_a(st, s):
                a, n = st.item(1), st.buf(1)
                p, kc = divmod(s, 2)
                if s % 8 == 0:
                    pe.wait_ge(mrow_in[s // 8], 32 * (a + 1))
                if some(16 * a + s - 1):
                    pe.wait_ge(exp_done, 16 * a + s - 1)
                pe.matmul(ST[s % 2][:, :], ks[n][:, p // 2, 128 * kc:128 * kc + 128],
                          qm[n][:, 2 * p:2 * p + 2, :], start=True, stop=True).then_inc(st_mm, 1)

            def values(a, n, q):
                pe.wait_ge(exp_done, 16 * a + 4 * q + 4)
                if q == 0:
                    pe.wait_ge(v_done, a + 1)
                if q % 2 == 0:
                    if some(2 * a + q // 2):
                        pe.wait_ge(av_sb, 2 * a + q // 2)
                for kc in range(2):
                    for i in range(4):
                        mm = pe.matmul(AV[32 * i:32 * i + 32, L * (q % 2):L * (q % 2) + L],
                                       vt[n][:, kc, 4 * q + i, :],
                                       probs[:, (4 * q + 2 * (i // 2) + kc) % 8, L * (i % 2):L * (i % 2) + L],
                                       start=(kc == 0), stop=(kc == 1))
                mm.then_inc(av_mm, 1)

            def gate_up(st, f, u):
                j, up = divmod(u, 2)
                if u == 0:
                    pe.wait_ge(hTl_done, f + 1)
                last = j - 1 if st.new else j - 2
                if last >= 0:
                    pe.wait_ge(act_done if up else tmp_done, 4 * f + last + 1)
                elif j == 0 and up and some(f):
                    pe.wait_ge(y_done, f)
                c0, width = gate_up_columns(j, up)
                n = 0
                for kc in range(2):
                    for lhs, rhs in ((hTh, wguh), (hTh, wgul), (hTl, wguh)):
                        mm = pe.matmul((up_bank if up else gate_bank)(st, j)[:, 0:width], lhs[:, kc, :], rhs[:, kc, c0:c0 + width],
                                       start=(n == 0), stop=(n == 5))
                        n += 1
                mm.then_inc(gu_mm, 1)

            def act_turn(f, k):
                pe.wait_ge(act_done, 4 * f + (2, 3, 4, 4)[k])
                n = min(4, NC - 4 * k)
                for c in range(4 * k, 4 * k + n):
                    mm = pe.transpose(turned[k][:, 128 * (c % 4):128 * (c % 4) + 128],
                                      act_[:, 128 * c:128 * c + 128], ident)
                mm.then_inc(act_t, 1)

            def attention_turn(c, tc):
                pe.wait_ge(av_sb, 2 * c + 2)
                for q in range(GROUPS):
                    mm = pe.transpose(M1[:, 128 * q:128 * q + 128], avsb[:, q, 128 * tc:128 * tc + 128], ident)
                mm.then_inc(av_t, 1)

            def attention_back(c):
                pe.wait_ge(a_norm, 2 * c + 2)
                for tc in range(2):
                    mm = pe.transpose(G[:, 128 * tc:128 * tc + 128],
                                      aT[:, tc, :, :].rearrange("p h d -> p (h d)"), ident)
                mm.then_inc(a_back, 1)

            def h_turn(c):
                pe.wait_ge(h_done, c + 1)
                for kc in range(2):
                    mm = pe.transpose(G[:, 128 * kc:128 * kc + 128], h[:, 128 * kc:128 * kc + 128], ident)
                mm.then_inc(h_t, 1)

            def down(st, f, c0, c1):
                if c0 == 0:
                    pe.wait_ge(act_done, 4 * f + (4 if st.new else 3))
                for c in range(c0, c1):
                    if c % 4 == 0:
                        pe.wait_ge(aTl_done, 4 * f + c // 4 + 1)
                    K = min(128, F - 128 * c)
                    for n, (lhs, rhs) in enumerate(((aTh, wdh), (aTh, wdl), (aTl, wdh))):
                        mm = pe.matmul(GU[:, 1, 0:L], lhs[0:K, c, :], rhs[0:K, c, :],
                                       start=(c == 0 and n == 0), stop=(c == NC - 1 and n == 2))
                if c1 == NC:
                    mm.then_inc(y_mm, 1)

            pe.wait_ge(const_in, 16)
            values_at = (1, 4, 9, 13)

            def step(st):
                b, a, c, g = (st.item(lag) for lag in range(4))
                if st.filling == 1:
                    pe.wait_ge(filled, 2)
                if st.ffn and not some(g):
                    pe.wait_ge(w_lo, by_vector(NW - 1))
                    pe.wait_ge(w_lo_pool, len(by_gpsimd))
                for s in range(SLOTS):
                    if st.new and s - 1 not in values_at:
                        scores_n(st, s)
                    if st.att:
                        scores_a(st, s)
                    if st.new and s in values_at:
                        scores_n(st, s + 1)
                    if st.att and s in values_at[1:]:
                        values(a, st.buf(1), values_at.index(s) - 1)
                    if st.comb and s == values_at[0]:
                        values(c, st.buf(2), 3)
                    if st.ffn and s in (0, 1, 2, 3, 5, 6, 7, 8):
                        gate_up(st, g, (0, 1, 2, 3, 5, 6, 7, 8).index(s))
                    if st.ffn and s >= 10:
                        down(st, g, *((0, 1), (1, 3), (3, 6), (6, 8), (8, 11), (11, NC))[s - 10])
                    if s == 1 and st.att:
                        if st.ffn and some(4 * g):
                            pe.wait_ge(aTl_done, 4 * g)
                        elif some(2 * c):
                            pe.wait_ge(a_norm, 2 * c)
                        elif some(2 * a):
                            pe.wait_ge(mrow_sb, 2 * a)
                        mrow_turn(a, 1)
                    if s == 3 and st.comb:
                        if st.att:
                            pe.wait_ge(mrow_sb, 2 * a + 2)
                        else:
                            pe.wait_ge(aTl_done, 4 * g)
                        attention_turn(c, 0)
                    if s == 5 and st.comb:
                        pe.wait_ge(a_norm, 2 * c + 1)
                        attention_turn(c, 1)
                    if s == 7 and st.ffn:
                        if st.comb:
                            pe.wait_ge(a_norm, 2 * c + 2)
                        else:
                            pe.wait_ge(aTl_done, 4 * g)
                        act_turn(g, 0)
                    if s == 10 and st.ffn:
                        pe.wait_ge(aTl_done, 4 * g + 1)
                        act_turn(g, 1)
                    if s == 12 and st.ffn:
                        pe.wait_ge(aTl_done, 4 * g + 2)
                        act_turn(g, 3)
                    if s == 9:
                        if st.ffn:
                            pe.wait_ge(tmp_done, 4 * g + 4)
                        elif some(2 * b - 1):
                            pe.wait_ge(mrow_sb, 2 * b - 1)
                        if st.new:
                            mrow_turn(b, 0)
                        if st.comb:
                            attention_back(c)
                    if s == 11 and st.ffn:
                        if st.comb:
                            pe.wait_ge(x1_done, c + 1)
                        if st.new:
                            pe.wait_ge(mrow_sb, 2 * b + 1)
                        act_turn(g, 2)
                    if s == 13 and st.comb:
                        if st.ffn:
                            pe.wait_ge(aTl_done, 4 * g + 3)
                        h_turn(c)

            steps(pe, step)


def constants():
    import numpy as np

    c = np.zeros((128, C_ALL), np.float32)
    c[:, C_ID:C_ID + 128] = np.eye(128)
    for i in range(4):
        c[:, C_MASK + i] = (np.arange(128) % 32) // CH == i
    c[:, C_L4:C_L4 + 16] = np.tril(np.ones((4, 4)), -1).reshape(1, 16)
    c[:, C_L8:C_L8 + 64] = np.tril(np.ones((8, 8)), -1).reshape(1, 64)
    return c


def kernel(x, ctx_2048, g_xattn, g_ffn, L0_ffn_gate_weight, L0_ffn_gate_w, L0_ffn_up_w, L0_ffn_down_w,
           L0_ffn_sh_gate_w, L0_ffn_sh_up_w, L0_ffn_sh_down_w):
    import numpy as np
    import concourse.bacc as bacc
    from concourse.bass_utils import run_bass_kernel_spmd

    a = np.asarray
    gate = np.concatenate([a(L0_ffn_sh_gate_w), a(L0_ffn_gate_w).reshape(-1, L)]).T
    up = np.concatenate([a(L0_ffn_sh_up_w), a(L0_ffn_up_w).reshape(-1, L)]).T
    cols = []
    for j, (first, width) in enumerate(zip(FIRST, BLOCKS)):
        cols.append(gate[:, first:first + width])
        if j == 0:
            cols.append(a(L0_ffn_gate_weight).T)
        cols.append(up[:, first:first + width])
    wd = np.zeros((FPAD, L), np.float32)
    wd[0:FS] = a(L0_ffn_sh_down_w).T
    wd[FS:F] = a(L0_ffn_down_w).transpose(0, 2, 1).reshape(-1, L)
    arrays = {
        "x": a(x),
        "y": a(ctx_2048),
        "yT": np.ascontiguousarray(a(ctx_2048).transpose(0, 2, 1)),
        "gx": a(g_xattn),
        "gf": a(g_ffn),
        "wgu": np.ascontiguousarray(np.concatenate(cols, axis=1)),
        "wd": wd,
        "consts": constants(),
    }
    nc = bacc.Bacc("TRN2", target_bir_lowering=False, num_devices=1)
    args = [nc.dram_tensor(n, v.shape, mybir.dt.from_np(v.dtype), kind="ExternalInput").ap()
            for n, v in arrays.items()]
    out = nc.dram_tensor("out", (B, W, L), F32, kind="ExternalOutput").ap()
    flamingo_kernel(nc, *args, out)
    r = run_bass_kernel_spmd(nc, [arrays], core_ids=[0])
    return r.results[0]["out"]
```
